# Optimizing a Trainium2 kernel written in Bass

```python
import numpy as np
import jax
import jax.numpy as jnp

def _softmax(x, axis=-1):
    return jax.nn.softmax(x, axis=axis)

def _gelu(x):
    return jax.nn.gelu(x, approximate=True)

def _silu(x):
    return jax.nn.silu(x)

def _sigmoid(x):
    return jax.nn.sigmoid(x)

def _layernorm(x, axis=-1, eps=1e-05):
    m = jnp.mean(x, axis=axis, keepdims=True)
    v = jnp.var(x, axis=axis, keepdims=True)
    return (x - m) / jnp.sqrt(v + eps)

def _scatter_add(tgt, idx, src, axis=0):
    return tgt.at[idx].add(src)

def _segment_sum(src, seg, n):
    return jax.ops.segment_sum(src, seg, n)
kernel_name = 'mk_gnn_preln_d1_gnn_r64_b75b6d'

def setup_inputs(seed: int=0):
    np.random.seed(seed)
    _w = jnp.asarray

    def _rec_inputs():
        import jax
        import jax.numpy as jnp
        _gk = jax.random.key(seed)
        x = -0.000202 + 1 * jax.random.normal(jax.random.fold_in(_gk, 1), (100000, 128), jnp.float32)
        src = jax.random.randint(jax.random.fold_in(_gk, 2), (50000,), 0, 100000, jnp.int32)
        dst = jax.random.randint(jax.random.fold_in(_gk, 3), (50000,), 0, 100000, jnp.int32)
        _o = jnp.argsort(dst, stable=True)
        src = src[_o]
        dst = dst[_o]
        edge_type_4 = jax.random.randint(jax.random.fold_in(_gk, 12), (50000,), 0, 4, jnp.int32)
        return (x, src, dst, edge_type_4)
    x, src, dst, edge_type_4 = _rec_inputs()

    def _L0_gnn_setup():
        import jax, jax.numpy as jnp
        import numpy as np
        N_NODES = 50000
        N_EDGES = 10000
        HIDDEN = 128
        EDGE_TYPES = 4
        key = jax.random.key(seed)
        ks = jax.random.split(key, 12)
        H, T = (HIDDEN, EDGE_TYPES)
        s1 = 1.0 / np.sqrt(2 * H)
        s2 = 1.0 / np.sqrt(H)
        return {'x': jax.random.normal(ks[0], (N_NODES, H), dtype=jnp.float32), 'edge_index': jax.random.randint(ks[1], (2, N_EDGES), 0, N_NODES, dtype=jnp.int64), 'edge_type': jax.random.randint(ks[2], (N_EDGES,), 0, T, dtype=jnp.int64), 'W1': jax.random.uniform(ks[3], (T, 2 * H, H), jnp.float32, -s1, s1), 'b1': jax.random.uniform(ks[4], (T, H), jnp.float32, -s1, s1), 'W2': jax.random.uniform(ks[5], (T, H, H), jnp.float32, -s2, s2), 'b2': jax.random.uniform(ks[6], (T, H), jnp.float32, -s2, s2), 'W_ih': jax.random.uniform(ks[7], (3 * H, H), jnp.float32, -s2, s2), 'W_hh': jax.random.uniform(ks[8], (3 * H, H), jnp.float32, -s2, s2), 'b_ih': jax.random.uniform(ks[9], (3 * H,), jnp.float32, -s2, s2), 'b_hh': jax.random.uniform(ks[10], (3 * H,), jnp.float32, -s2, s2)}
    _L0_gnn_all = _L0_gnn_setup()
    _L0_gnn_in = {k: v for k, v in _L0_gnn_all.items() if k in ('W1', 'b1', 'W2', 'b2', 'W_ih', 'W_hh', 'b_ih', 'b_hh')}
    del _L0_gnn_all
    return {'x': x, 'src': src, 'dst': dst, 'edge_type_4': edge_type_4, 'L0_gnn_W1': _L0_gnn_in['W1'], 'L0_gnn_b1': _L0_gnn_in['b1'], 'L0_gnn_W2': _L0_gnn_in['W2'], 'L0_gnn_b2': _L0_gnn_in['b2'], 'L0_gnn_W_ih': _L0_gnn_in['W_ih'], 'L0_gnn_W_hh': _L0_gnn_in['W_hh'], 'L0_gnn_b_ih': _L0_gnn_in['b_ih'], 'L0_gnn_b_hh': _L0_gnn_in['b_hh']}

def reference(x, src, dst, edge_type_4, L0_gnn_W1, L0_gnn_b1, L0_gnn_W2, L0_gnn_b2, L0_gnn_W_ih, L0_gnn_W_hh, L0_gnn_b_ih, L0_gnn_b_hh):
    import jax
    import jax.numpy as jnp

    def _L0_gnn_ref(x, edge_index, edge_type, W1, b1, W2, b2, W_ih, W_hh, b_ih, b_hh):
        import jax, jax.numpy as jnp
        import numpy as np
        N_NODES = 50000
        N_EDGES = 10000
        HIDDEN = 128
        EDGE_TYPES = 4
        num_nodes = x.shape[0]
        src, dst = (edge_index[0], edge_index[1])
        msg_input = jnp.concatenate([x[src], x[dst]], axis=1)
        n_types = W1.shape[0]
        msgs = jnp.zeros((msg_input.shape[0], x.shape[1]), dtype=x.dtype)
        for t in range(n_types):
            h = jax.nn.relu(msg_input @ W1[t] + b1[t])
            m = h @ W2[t] + b2[t]
            msgs = msgs + jnp.where((edge_type == t)[:, None], m, jnp.zeros((), x.dtype))
        agg = jax.ops.segment_sum(msgs, dst, num_segments=num_nodes)
        gi = agg @ W_ih.T + b_ih
        gh = x @ W_hh.T + b_hh
        i_r, i_z, i_n = jnp.split(gi, 3, axis=1)
        h_r, h_z, h_n = jnp.split(gh, 3, axis=1)
        r = jax.nn.sigmoid(i_r + h_r)
        z = jax.nn.sigmoid(i_z + h_z)
        n = jnp.tanh(i_n + r * h_n)
        return (1.0 - z) * n + z * x
    edge_index = jnp.stack([src, dst])
    h = jnp.maximum(_layernorm(x, axis=-1), 0.0)
    x = x + _L0_gnn_ref(h, edge_index, edge_type_4, L0_gnn_W1, L0_gnn_b1, L0_gnn_W2, L0_gnn_b2, L0_gnn_W_ih, L0_gnn_W_hh, L0_gnn_b_ih, L0_gnn_b_hh)
    return x

_drawn_inputs = setup_inputs


def setup_inputs(seed=0):
    import zlib

    import numpy as np

    out = dict(_drawn_inputs(seed))
    spreads = {}
    factors = {'L0_gnn_b1': 27.024, 'L0_gnn_b2': 6.062, 'L0_gnn_b_hh': 4.909, 'L0_gnn_b_ih': 2.683}
    for name, (base, spread) in spreads.items():
        noise = np.random.default_rng([zlib.crc32(name.encode()), seed]).standard_normal(out[name].shape)
        drawn = base * np.exp(spread * noise) if base else spread * noise
        out[name] = jnp.asarray(drawn.astype(out[name].dtype))
    for name, factor in factors.items():
        out[name] = (out[name] * factor).astype(out[name].dtype)
    return out
```

```python
from contextlib import ExitStack

import concourse.bass as bass
from concourse import mybir

F32 = mybir.dt.float32
F32R = mybir.dt.float32r
BF16 = mybir.dt.bfloat16
I32 = mybir.dt.int32
ALU = mybir.AluOpType
ACT = mybir.ActivationFunctionType
AX_X = mybir.AxisListType.X

P = 128
D = 128
TYPES = 4
TILES = 4
GROUP = TILES * P
EPS = 1e-5
BIG = float(2 ** 100)
UNROLL = 4
HEAD = 8
BUCKETS = 32
PITCH = 144
ROW = D + 1


def groups_of(rows):
    return -(-rows // GROUP)


def due(value):
    return not isinstance(value, int) or value > 0


def within(g, count):
    return not isinstance(g, int) or 0 <= g < count


def uses(g, slot, ring, inc):
    return (g - slot) * (inc // ring) + inc


def pipeline(eng, count, first, last, step):
    end = (count - UNROLL) // UNROLL * UNROLL
    for i in range(first, HEAD):
        step(i, i % UNROLL)
    with eng.Fori(HEAD, end - UNROLL + 1, UNROLL) as i:
        for j in range(UNROLL):
            step(i + j, j)
    for i in range(end, count + last):
        step(i, i % UNROLL)


def gnn_layer(nc, x, edge_rows, dst_cols, types, W1, b1, W2, b2, WihT, WhhT, b_ih, b_hh, out):
    NODES = x.shape[0]
    NG = groups_of(NODES)
    EG = edge_rows.shape[1]
    ECOLS = EG * TILES
    EROWS = ECOLS * P

    messages = nc.dram_tensor("messages", (EROWS, PITCH), F32, kind="Internal").ap()
    starts_dram = nc.dram_tensor("starts", (BUCKETS * BUCKETS,), I32, kind="Internal").ap()

    ctx = ExitStack()
    with ctx:
        def sb(name, shape, dt=F32):
            return ctx.enter_context(nc.sbuf_tensor(name, shape, dt))

        def sem(name):
            return ctx.enter_context(nc.semaphore(name))

        iota_i = sb("iota_i", [P, P], I32)
        iota = sb("iota", [P, P])
        part_i = sb("part_i", [P, 3], I32)
        part = sb("part", [P, 3])
        ident = sb("ident", [P, P])
        tile_base_i = sb("tile_base_i", [P, NG * TILES], I32)
        tile_base = sb("tile_base", [P, NG * TILES])
        power = sb("power", [P, 2 * TILES])
        gathers_may_start = sb("gathers_may_start", [1, 1])
        ones32 = sb("ones32", [P, BUCKETS])
        w1 = sb("w1", [P, TYPES * 2 * D])
        w1_hi = sb("w1_hi", [P, TYPES * 2 * D], F32R)
        w1_lo = sb("w1_lo", [P, TYPES * 2 * D], F32R)
        w2 = sb("w2", [P, TYPES * D])
        w2_hi = sb("w2_hi", [P, TYPES * D], F32R)
        w2_lo = sb("w2_lo", [P, TYPES * D], F32R)
        wih = sb("wih", [P, 3 * D])
        whh = sb("whh", [P, 3 * D])
        whh_hi = sb("whh_hi", [P, 3 * D], F32R)
        whh_lo = sb("whh_lo", [P, 3 * D], F32R)
        bih = sb("bih", [P, 3])
        bhh = sb("bhh", [P, 3])
        bsum = sb("bsum", [P, 3])
        bneg = sb("bneg", [P, 3])
        bias = sb("bias", [2 * TYPES, 2, D])
        bias_hi = sb("bias_hi", [2 * TYPES, 2, D], F32R)
        bias_lo = sb("bias_lo", [2 * TYPES, 2, D], F32R)
        bias_parts = sb("bias_parts", [2 * TYPES, 2, D])
        bias1 = sb("bias1", [2 * TYPES, TYPES, D], F32R)
        bias2 = sb("bias2", [2 * TYPES, D], F32R)
        r4_i = sb("r4_i", [2 * TYPES, 1], I32)
        r4 = sb("r4", [2 * TYPES, 1])
        upper = sb("upper", [2 * TYPES, 2])
        pick = sb("pick", [2 * TYPES, TYPES])
        minus_big = sb("minus_big", [2 * TYPES, TYPES])

        dst_i = sb("dst_i", [P, ECOLS], I32)
        dst_f = sb("dst_f", [P, ECOLS])
        q_i = sb("q_i", [P, 2, ECOLS], I32)
        q_f = sb("q_f", [P, 2, ECOLS])
        block_mask = sb("block_mask", [P, 4])
        hist4 = sb("hist4", [P, 4, BUCKETS])
        hist = sb("hist", [P, BUCKETS])
        hist_upto = sb("hist_upto", [P, BUCKETS])
        hist_before = sb("hist_before", [P, BUCKETS])
        hist_total = sb("hist_total", [P, BUCKETS])
        same_high = sb("same_high", [P, BUCKETS])
        later_high = sb("later_high", [P, BUCKETS])
        starts_i = sb("starts_i", [BUCKETS, BUCKETS], I32)
        starts = sb("starts_row", [1, BUCKETS * BUCKETS], I32)

        rows_all = sb("rows_all", [P, EG, 2 * TILES], I32)
        rows_now = sb("rows_now", [P, 4, 2 * TILES], I32)
        e_x = sb("e_x", [P, 2, 2 * TILES, D])
        e_y = sb("e_y", [P, 2, 2 * TILES, D])
        e_h_hi = sb("e_h_hi", [P, 2, 2, GROUP], F32R)
        e_h_lo = sb("e_h_lo", [P, 2, 2, GROUP], F32R)
        e_r_hi = sb("e_r_hi", [P, 2, TYPES, GROUP], F32R)
        e_r_lo = sb("e_r_lo", [P, 2, TYPES, GROUP], F32R)
        e_type = sb("e_type", [2 * TYPES, 4, GROUP], I32)
        e_onehot = sb("e_onehot", [2 * TYPES, 4, GROUP], F32R)
        e_msg = sb("e_msg", [P, 4, TILES, ROW])

        bn = sb("bn", [P, 2 * TILES, 6])
        pair = sb("pair", [P, 2 * TILES, 2])
        diff = sb("diff", [P, 2 * TILES])
        mean = sb("mean", [P, 2 * TILES])
        quarter = sb("quarter", [P, 2 * TILES])
        within_half = sb("within_half", [P, 2 * TILES])
        var = sb("var", [P, 2 * TILES])
        rstd = sb("rstd", [P, 2 * TILES])

        n_all = sb("n_all", [P, ECOLS * BUCKETS])
        taken = [0]

        def carve(ring, width):
            at = taken[0]
            taken[0] += ring * width
            return n_all[:, at:at + ring * width].rearrange("p (r w) -> p r w", r=ring)

        n_x = e_x[:].rearrange("p a (b k) d -> p (a b) (k d)", b=2)
        n_xh = e_y[:].rearrange("p a (b k) d -> p (a b) (k d)", b=2)
        n_y = carve(2, GROUP)
        n_sel = carve(2, GROUP)
        n_agg = carve(2, GROUP)
        n_r = carve(2, GROUP)
        n_zc = carve(2, GROUP)
        n_t = carve(2, GROUP)
        n_n = carve(2, GROUP)
        n_d = carve(2, GROUP)
        n_e = carve(2, GROUP)
        n_out = carve(4, GROUP)
        n_win = sb("n_win", [P, 4, TILES, ROW])
        n_h_hi = e_r_hi[:, 0, 0:2, :]
        n_h_lo = e_r_lo[:, 0, 0:2, :]
        half = ECOLS * BUCKETS // 2
        high_1h = n_all[:, 0:half].bitcast(BF16).rearrange("p (c b) -> p c b", b=BUCKETS)
        low_1h = n_all[:, half:2 * half].bitcast(BF16).rearrange("p (c b) -> p c b", b=BUCKETS)

        bank = [ctx.enter_context(nc.psum_tensor(f"bank{b}", [P, GROUP], F32)) for b in range(8)]

        s_weights = sem("s_weights")
        s_rows = sem("s_rows")
        s_dst = sem("s_dst")
        s_iota = sem("s_iota")
        s_const = sem("s_const")
        s_power = sem("s_power")
        s_split_hi = sem("s_split_hi")
        s_split = sem("s_split")
        s_prep = sem("s_prep")
        s_onehot_hist = sem("s_onehot_hist")
        s_hist = sem("s_hist")
        s_hist_ops = sem("s_hist_ops")
        s_start_mm = sem("s_start_mm")
        s_starts_i = sem("s_starts_i")
        s_starts_out = sem("s_starts_out")
        s_starts = sem("s_starts")

        e_staged = sem("e_staged")
        e_gated = sem("e_gated")
        e_gathered = [sem(f"e_gathered{s}") for s in range(2)]
        e_typed = [sem(f"e_typed{s}") for s in range(4)]
        e_stored = [sem(f"e_stored{s}") for s in range(4)]
        ln_ops = sem("ln_ops")
        e_var = sem("e_var")
        e_rstd = sem("e_rstd")
        e_normed = sem("e_normed")
        e_turned = sem("e_turned")
        e_hhi = sem("e_hhi")
        e_hlo = sem("e_hlo")
        e_oh = sem("e_oh")
        e_l1 = sem("e_l1")
        e_rhi = sem("e_rhi")
        e_rlo = sem("e_rlo")
        e_l2 = sem("e_l2")
        e_msged = sem("e_msged")
        e_dsted = sem("e_dsted")

        n_loaded = [sem(f"n_loaded{s}") for s in range(4)]
        n_windowed = [sem(f"n_windowed{s}") for s in range(4)]
        n_stored = [sem(f"n_stored{s}") for s in range(4)]
        n_var = sem("n_var")
        n_rstd = sem("n_rstd")
        n_normed = sem("n_normed")
        n_seled = sem("n_seled")
        n_relued = sem("n_relued")
        n_xhed = sem("n_xhed")
        n_turned = sem("n_turned")
        n_summed = sem("n_summed")
        n_hhi = sem("n_hhi")
        n_hlo = sem("n_hlo")
        n_agged = sem("n_agged")
        n_gate = sem("n_gate")
        n_red = sem("n_red")
        n_zed = sem("n_zed")
        n_ted = sem("n_ted")
        n_ued = sem("n_ued")
        n_ned = sem("n_ned")
        n_ded = sem("n_ded")
        n_eed = sem("n_eed")
        n_back = sem("n_back")
        n_outed = sem("n_outed")

        N_WEIGHTS = 10
        N_SPLITS = 4
        LN_STEPS = 3
        block = ctx.enter_context(nc.Block())

        @block.sync
        def _(sp):
            sp.dma_start(rows_all[:], edge_rows).then_inc(s_rows, 16)
            sp.dma_start(dst_i[:], dst_cols).then_inc(s_dst, 16)
            sp.dma_start(w1[:].rearrange("p (t k o) -> p t k o", t=TYPES, k=2),
                         W1.rearrange("t (k p) o -> p t k o", p=P)).then_inc(s_weights, 16)
            sp.dma_start(w2[:].rearrange("p (t o) -> p t o", t=TYPES),
                         W2.rearrange("t p o -> p t o")).then_inc(s_weights, 16)
            sp.dma_start(wih[:], WihT).then_inc(s_weights, 16)
            sp.dma_start(whh[:], WhhT).then_inc(s_weights, 16)
            sp.dma_start(bih[:], b_ih).then_inc(s_weights, 16)
            sp.dma_start(bhh[:], b_hh).then_inc(s_weights, 16)
            for copy in range(2):
                sp.dma_start(bias[copy * TYPES:(copy + 1) * TYPES, 0, :], b1).then_inc(s_weights, 16)
                sp.dma_start(bias[copy * TYPES:(copy + 1) * TYPES, 1, :], b2).then_inc(s_weights, 16)

            def edge_io(i, m):
                g, s = i + 2, (m + 2) % 4
                if within(g, EG):
                    if due(g - 3):
                        sp.wait_ge(e_oh, g - 3)
                    sp.dma_start(e_type[:, s, :], types[:, bass.ds(g * GROUP, GROUP)]
                                 .to_broadcast([2 * TYPES, GROUP])).then_inc(e_typed[s], 16)
                g, s = i - 2, (m - 2) % 4
                if within(g, EG):
                    sp.wait_ge(e_msged, g + 1)
                    sp.wait_ge(e_dsted, g + 1)
                    sp.dma_start(messages[bass.ds(g * GROUP, GROUP), 0:ROW].rearrange("(k p) d -> p k d", p=P),
                                 e_msg[:, s]).then_inc(e_stored[s], 16)

            pipeline(sp, EG, -2, 2, edge_io)
            for s in range(4):
                sp.wait_ge(e_stored[s], uses((EG - 1 - s) // 4 * 4 + s, s, 4, 16))
            sp.wait_ge(s_starts_i, 1)
            sp.dma_start(starts_dram.rearrange("(h l) -> h l", l=BUCKETS), starts_i[:]).then_inc(s_starts_out, 16)
            sp.wait_ge(s_starts_out, 16)
            sp.dma_start(starts[:], starts_dram.rearrange("(a n) -> a n", a=1)).then_inc(s_starts, 16)
            sp.wait_ge(s_starts, 16)

            TAIL = NODES - (NG - 1) * GROUP
            parts = [(k, min(P, TAIL - k * P)) for k in range(TILES) if TAIL > k * P]

            def node_io(i, m):
                g, s = i + 3, (m + 3) % 4
                if within(g, NG):
                    if due(g - 3):
                        sp.wait_ge(n_normed, g - 3)
                        sp.wait_ge(n_xhed, g - 3)
                    if isinstance(g, int) and g == NG - 1:
                        for k, rows in parts:
                            sp.dma_start(n_x[0:rows, s, k * D:(k + 1) * D],
                                         x[g * GROUP + k * P:g * GROUP + k * P + rows, :]).then_inc(n_loaded[s], 16)
                    else:
                        sp.dma_start(n_x[:, s, :].rearrange("p (k d) -> p k d", k=TILES),
                                     x[bass.ds(g * GROUP, GROUP), :].rearrange("(k p) d -> p k d", p=P)
                                     ).then_inc(n_loaded[s], 16)
                    if due(g - 3):
                        sp.wait_ge(n_summed, g - 3)
                    for k in range(TILES):
                        start = sp.value_load(starts[0:1, bass.ds(g * TILES + k, 1)],
                                              min_val=0, max_val=EROWS - P)
                        sp.dma_start(n_win[:, s, k, :], messages[bass.ds(start, P), 0:ROW]
                                     ).then_inc(n_windowed[s], 16)
                g, s = i - 2, (m - 2) % 4
                if within(g, NG):
                    sp.wait_ge(n_outed, g + 1)
                    if isinstance(g, int) and g == NG - 1:
                        for k, rows in parts:
                            sp.dma_start(out[g * GROUP + k * P:g * GROUP + k * P + rows, :],
                                         n_out[0:rows, s, k * D:(k + 1) * D]).then_inc(n_stored[s], 16)
                    else:
                        sp.dma_start(out[bass.ds(g * GROUP, GROUP), :].rearrange("(k p) d -> p k d", p=P),
                                     n_out[:, s, :].rearrange("p (k d) -> p k d", k=TILES)
                                     ).then_inc(n_stored[s], 16)

            sp.wait_ge(s_hist, 1)
            pipeline(sp, NG, -3, 2, node_io)
            for s in range(4):
                last = (NG - 1 - s) // 4 * 4 + s
                extra = 16 * (len(parts) - 1) if last == NG - 1 else 0
                sp.wait_ge(n_stored[s], uses(last, s, 4, 16) + extra)

        @block.gpsimd
        def _(pool):
            nc.gpsimd.iota(iota_i[:], pattern=[[1, P]], base=0, channel_multiplier=0)
            nc.gpsimd.iota(tile_base_i[:], pattern=[[P, NG * TILES]], base=0, channel_multiplier=0)
            nc.gpsimd.iota(part_i[:, 0:1], pattern=[[0, 1]], base=0, channel_multiplier=1).then_inc(s_iota, 1)

            nc.gpsimd.memset(power[:], -0.5).then_inc(s_power, 1)
            pool.wait_ge(s_power, 1)

            def stage(g, s):
                nc.gpsimd.tensor_copy(rows_now[:, s, :], rows_all[:, bass.ds(g, 1), :]
                                      .rearrange("p a k -> p (a k)")).then_inc(e_staged, 1)

            pool.wait_ge(s_rows, 16)
            stage(0, 0)

            def edge_rstd(g):
                pool.wait_ge(e_var, g + 1)
                nc.gpsimd.tensor_tensor(rstd[:], var[:], power[:], ALU.pow).then_inc(e_rstd, 1)

            def gather(g, m):
                if within(g + 1, EG):
                    stage(g + 1, (m + 1) % 4)
                pool.wait_ge(e_staged, g + 1)
                if due(g):
                    pool.wait_ge(e_gated, g)
                if due(g - 1):
                    pool.wait_ge(e_normed, g - 1)
                nc.gpsimd.tensor_tensor(gathers_may_start[:], power[0:1, 0:1], power[0:1, 0:1],
                                        ALU.add).then_inc(e_gated, 1)
                for k in range(2 * TILES):
                    if k == 5 and within(g - 1, EG):
                        edge_rstd(g - 1)
                    nc.gpsimd.indirect_dma_start(
                        e_x[:, m % 2, k, :], None, x,
                        bass.IndirectOffsetOnAxis(ap=rows_now[:, m % 4, k:k + 1], axis=0)
                    ).then_inc(e_gathered[m % 2], 16)

            pipeline(pool, EG, 0, 0, gather)
            edge_rstd(EG - 1)

            def node_side(i, m):
                g, s = i + 1, (m + 1) % 4
                if within(g, NG):
                    pool.wait_ge(n_normed, g + 1)
                    if due(g - 3):
                        pool.wait_ge(n_outed, g - 3)
                g, s = i - 1, (m - 1) % 2
                if within(g, NG):
                    pool.wait_ge(n_ded, g + 1)
                    pool.wait_ge(n_zed, g + 1)
                    if due(g - 1):
                        pool.wait_ge(n_back, g - 1)
                    nc.gpsimd.tensor_tensor(n_e[:, s, :], n_d[:, s, :], n_zc[:, s, :], ALU.mult).then_inc(n_eed, 1)
                g, s = i + 1, (m + 1) % 4
                if within(g, NG):
                    nc.gpsimd.tensor_scalar(n_xh[:, s, :], n_y[:, s % 2, :], 0.0, None,
                                            ALU.max).then_inc(n_relued, 1)
                    pool.wait_ge(n_relued, g + 1)
                    nc.gpsimd.tensor_tensor(n_xh[:, s, :], n_xh[:, s, :], n_x[:, s, :], ALU.add).then_inc(n_xhed, 1)
                g = i + 2
                if within(g, NG):
                    pool.wait_ge(n_var, g + 1)
                    nc.gpsimd.tensor_tensor(rstd[:, 0:TILES], var[:, 0:TILES], power[:, 0:TILES],
                                            ALU.pow).then_inc(n_rstd, 1)

            pool.wait_ge(s_hist, 1)
            pipeline(pool, NG, -2, 1, node_side)

        @block.vector
        def _(dve):
            chain = [0]

            def link(ins):
                chain[0] += 1
                ins.then_inc(s_prep, 1)
                dve.wait_ge(s_prep, chain[0])

            V = nc.vector
            dve.wait_ge(s_iota, 1)
            V.tensor_copy(iota[:], iota_i[:])
            V.tensor_copy(tile_base[:], tile_base_i[:])
            V.tensor_scalar(part_i[:, 1:2], part_i[:, 0:1], 5, None, ALU.arith_shift_right)
            V.memset(ones32[:], 1.0)
            V.tensor_scalar(r4_i[:], part_i[0:2 * TYPES, 0:1], TYPES - 1, None, ALU.bitwise_and)
            link(V.tensor_scalar(part_i[:, 2:3], part_i[:, 0:1], BUCKETS - 1, None, ALU.bitwise_and))
            V.tensor_copy(r4[:], r4_i[:])
            link(V.tensor_copy(part[:], part_i[:]))
            V.tensor_scalar(block_mask[:], iota[:, 0:4], part[:, 1:2], None, ALU.is_equal)
            V.tensor_scalar(same_high[:], iota[:, 0:BUCKETS], part[:, 2:3], None, ALU.is_equal)
            V.tensor_scalar(later_high[:], iota[:, 0:BUCKETS], part[:, 2:3], None, ALU.is_gt)
            V.tensor_scalar(pick[:], iota[0:2 * TYPES, 0:TYPES], r4[:], None, ALU.is_equal)
            V.tensor_scalar(upper[:, 0:1], part[0:2 * TYPES, 0:1], float(TYPES), None, ALU.is_lt)
            V.tensor_scalar(upper[:, 1:2], part[0:2 * TYPES, 0:1], float(TYPES), None, ALU.is_ge)
            link(V.tensor_scalar(ident[:], iota[:], part[:, 0:1], None, ALU.is_equal))
            link(V.tensor_scalar(minus_big[:], pick[:], BIG, -BIG, ALU.mult, ALU.add))
            link(V.tensor_scalar(minus_big[:], minus_big[:], upper[:, 0:1], None, ALU.mult))
            dve.wait_ge(s_weights, 16 * N_WEIGHTS)
            dve.wait_ge(s_split_hi, N_SPLITS)
            V.tensor_tensor(w1_lo[:], w1[:], w1_hi[:].bitcast(F32), ALU.subtract)
            V.tensor_tensor(w2_lo[:], w2[:], w2_hi[:].bitcast(F32), ALU.subtract)
            V.tensor_tensor(whh_lo[:], whh[:], whh_hi[:].bitcast(F32), ALU.subtract)
            link(V.tensor_tensor(bias_lo[:], bias[:], bias_hi[:].bitcast(F32), ALU.subtract))
            link(V.tensor_scalar(bias_parts[:], bias_hi[:].bitcast(F32), upper[:, 0:1], None, ALU.mult))
            link(V.scalar_tensor_tensor(out=bias_parts[:], in0=bias_lo[:].bitcast(F32), scalar=upper[:, 1:2],
                                        in1=bias_parts[:], op0=ALU.mult, op1=ALU.add))
            V.tensor_copy(bias2[:], bias_parts[:, 1, :])
            for t in range(TYPES):
                V.tensor_scalar(bias1[:, t, :], bias_parts[:, 0, :], pick[:, t:t + 1], minus_big[:, t:t + 1],
                                ALU.mult, ALU.add)
            link(V.tensor_tensor(bsum[:], bih[:], bhh[:], ALU.add))
            V.tensor_scalar(bneg[:], bsum[:], -1.0, None, ALU.mult).then_inc(s_const, 1)

            dve.wait_ge(s_dst, 16)
            V.tensor_copy(dst_f[:], dst_i[:])
            V.tensor_scalar(q_i[:, 0, :], dst_i[:], 12, None, ALU.arith_shift_right)
            link(V.tensor_scalar(q_i[:, 1, :], dst_i[:], 7, BUCKETS - 1, ALU.arith_shift_right, ALU.bitwise_and))
            link(V.tensor_copy(q_f[:], q_i[:]))
            for n, onehot in enumerate((high_1h, low_1h)):
                last = V.tensor_tensor(onehot, iota[:, 0:BUCKETS].unsqueeze(1).to_broadcast([P, ECOLS, BUCKETS]),
                                       q_f[:, n, :].unsqueeze(2).to_broadcast([P, ECOLS, BUCKETS]), ALU.is_equal)
            last.then_inc(s_onehot_hist, 1)

            def ln_stats(count, base, tile, finish):
                done = [base]

                def ln_link(ins):
                    done[0] = done[0] + 1
                    ins.then_inc(ln_ops, 1)
                    dve.wait_ge(ln_ops, done[0])

                for k in range(count):
                    last = V.bn_stats(bn[:, k, :], tile(k))
                ln_link(last)
                halves = bn[:, 0:count, :].rearrange("p k (h c) -> p k h c", h=2)
                V.tensor_tensor(pair[:, 0:count, :], halves[:, :, 0, 1:3], halves[:, :, 1, 1:3], ALU.add)
                ln_link(V.tensor_tensor(diff[:, 0:count], bn[:, 0:count, 1], bn[:, 0:count, 4], ALU.subtract))
                V.tensor_scalar(mean[:, 0:count], pair[:, 0:count, 0], 0.5, None, ALU.mult)
                V.tensor_scalar(within_half[:, 0:count], pair[:, 0:count, 1], 1.0 / D, EPS, ALU.mult, ALU.add)
                ln_link(V.scalar_tensor_tensor(out=quarter[:, 0:count], in0=diff[:, 0:count], scalar=0.25,
                                               in1=diff[:, 0:count], op0=ALU.mult, op1=ALU.mult))
                V.tensor_tensor(var[:, 0:count], within_half[:, 0:count], quarter[:, 0:count],
                                ALU.add).then_inc(finish, 1)

            def ln_apply(count, tile, normed, finish):
                for k in range(count):
                    last = V.tensor_scalar(normed(k), tile(k), mean[:, k:k + 1], rstd[:, k:k + 1],
                                           ALU.subtract, ALU.mult)
                last.then_inc(finish, 1)

            def low_hidden(i, m, t):
                dve.wait_ge(e_rhi, 4 * i + t + 1)
                if t == 0 and due(i - 1):
                    dve.wait_ge(e_l2, i - 1)
                V.scalar_tensor_tensor(out=e_r_lo[:, m % 2, t, :], in0=bank[2 + t][:], scalar=0.0,
                                       in1=e_r_hi[:, m % 2, t, :].bitcast(F32), op0=ALU.max,
                                       op1=ALU.subtract).then_inc(e_rlo, 1)

            def edge_step(i, m):
                g, s = i + 1, (m + 1) % 4
                if within(g, EG):
                    for half_ in range(2):
                        dve.wait_ge(e_hhi, 2 * g + half_ + 1)
                        if half_ == 0 and due(g - 1):
                            dve.wait_ge(e_l1, 4 * (g - 1))
                        V.scalar_tensor_tensor(out=e_h_lo[:, s % 2, half_, :], in0=bank[half_][:], scalar=0.0,
                                               in1=e_h_hi[:, s % 2, half_, :].bitcast(F32), op0=ALU.max,
                                               op1=ALU.subtract).then_inc(e_hlo, 1)
                    dve.wait_ge(e_typed[s], uses(g, s, 4, 16))
                    if due(g - 3):
                        dve.wait_ge(e_l2, g - 3)
                    V.tensor_scalar(e_onehot[:, s, :], e_type[:, s, :], r4[:], None, ALU.is_equal).then_inc(e_oh, 1)
                g, s = i - 1, (m - 1) % 4
                if within(g, EG):
                    if due(g - 3):
                        dve.wait_ge(e_stored[s], uses(g - 4, s, 4, 16))
                    V.tensor_copy(e_msg[:, s, :, D:ROW].rearrange("p k a -> p (k a)"),
                                  dst_f[:, bass.ds(g * TILES, TILES)]).then_inc(e_dsted, 1)
                if within(i, EG):
                    low_hidden(i, m, 0)
                g, s = i + 2, (m + 2) % 2
                if within(g, EG):
                    dve.wait_ge(e_gathered[s], uses(g, s, 2, 16 * 2 * TILES))
                    if due(g - 1):
                        dve.wait_ge(e_turned, g - 1)
                    ln_stats(2 * TILES, g * LN_STEPS, lambda k: e_x[:, s, k, :], e_var)
                if within(i, EG):
                    low_hidden(i, m, 1)
                    low_hidden(i, m, 2)
                if within(g, EG):
                    dve.wait_ge(e_rstd, g + 1)
                    ln_apply(2 * TILES, lambda k: e_x[:, s, k, :], lambda k: e_y[:, s, k, :], e_normed)
                if within(i, EG):
                    low_hidden(i, m, 3)

            pipeline(dve, EG, -2, 1, edge_step)

            dve.wait_ge(s_hist, 1)
            done = [0]

            def hist_link(ins):
                done[0] += 1
                ins.then_inc(s_hist_ops, 1)
                dve.wait_ge(s_hist_ops, done[0])

            hist_link(V.tensor_tensor(hist4[:], bank[7][:, 0:P].rearrange("p (j l) -> p j l", j=4),
                                      block_mask[:].unsqueeze(2).to_broadcast([P, 4, BUCKETS]), ALU.mult))
            hist_link(V.tensor_reduce(hist[:], hist4[:].rearrange("p j l -> p l j"), AX_X, ALU.add))
            hist_link(V.tensor_tensor_scan(hist_upto[:], ones32[:], hist[:], 0.0, ALU.mult, ALU.add))
            V.tensor_tensor(hist_before[:], hist_upto[:], hist[:], ALU.subtract)
            hist_link(V.tensor_scalar(hist_total[:], ones32[:], hist_upto[:, BUCKETS - 1:BUCKETS], None, ALU.mult))
            dve.wait_ge(s_start_mm, 1)
            V.tensor_copy(starts_i[:], bank[7][0:BUCKETS, P:P + BUCKETS]).then_inc(s_starts_i, 1)

            def node_step(i, m):
                g, s = i - 2, (m - 2) % 4
                if within(g, NG):
                    dve.wait_ge(n_back, g + 1)
                    if due(g - 3):
                        dve.wait_ge(n_stored[s], uses(g - 4, s, 4, 16))
                    V.tensor_tensor(n_out[:, s, :], n_xh[:, s, :], bank[7][:], ALU.subtract).then_inc(n_outed, 1)
                g, s = i - 1, (m - 1) % 2
                if within(g, NG):
                    dve.wait_ge(n_ned, g + 1)
                    if due(g - 1):
                        dve.wait_ge(n_eed, g - 1)
                    V.scalar_tensor_tensor(out=n_d[:, s, :], in0=bank[s][:], scalar=0.0, in1=n_n[:, s, :],
                                           op0=ALU.max, op1=ALU.subtract).then_inc(n_ded, 1)
                g, s = i + 2, (m + 2) % 4
                if within(g, NG):
                    tail = isinstance(g, int) and g == NG - 1
                    dve.wait_ge(n_loaded[s], uses(g, s, 4, 16) + (16 * (-(-(NODES - g * GROUP) // P) - 1) if tail else 0))
                    if due(g - 1):
                        dve.wait_ge(n_turned, g - 1)
                        dve.wait_ge(n_xhed, g - 1)
                    ln_stats(TILES, EG * LN_STEPS + g * LN_STEPS, lambda k: n_x[:, s, k * D:(k + 1) * D], n_var)
                if within(g, NG):
                    dve.wait_ge(n_windowed[s], uses(g, s, 4, 64))
                    if due(g - 1):
                        dve.wait_ge(n_summed, g - 1)
                    for k in range(TILES):
                        last = V.tensor_scalar(n_sel[:, s % 2, k * P:(k + 1) * P], iota[:],
                                               tile_base[:, bass.ds(g * TILES + k, 1)], n_win[:, s, k, D:ROW],
                                               ALU.add, ALU.is_equal)
                    last.then_inc(n_seled, 1)
                g, s = i, m % 2
                if within(g, NG):
                    dve.wait_ge(n_red, g + 1)
                    dve.wait_ge(n_gate, 4 * g + 2)
                    if due(g - 1):
                        dve.wait_ge(n_ned, g - 1)
                    V.scalar_tensor_tensor(out=n_t[:, s, :], in0=bank[4][:], scalar=bhh[:, 2:3], in1=n_r[:, s, :],
                                           op0=ALU.add, op1=ALU.mult).then_inc(n_ted, 1)
                g, s = i + 1, (m + 1) % 2
                if within(g, NG):
                    dve.wait_ge(n_hhi, g + 1)
                    if due(g - 1):
                        dve.wait_ge(n_gate, 4 * (g - 1))
                    V.scalar_tensor_tensor(out=n_h_lo[:, s, :], in0=bank[s][:], scalar=0.0,
                                           in1=n_h_hi[:, s, :].bitcast(F32), op0=ALU.max,
                                           op1=ALU.subtract).then_inc(n_hlo, 1)
                g, s = i, m % 2
                if within(g, NG):
                    dve.wait_ge(n_gate, 4 * g + 3)
                    dve.wait_ge(n_ted, g + 1)
                    V.tensor_tensor(n_t[:, s, :], bank[5][:], n_t[:, s, :], ALU.add).then_inc(n_ued, 1)
                g, s = i + 2, (m + 2) % 4
                if within(g, NG):
                    dve.wait_ge(n_rstd, g + 1)
                    ln_apply(TILES, lambda k: n_x[:, s, k * D:(k + 1) * D],
                             lambda k: n_y[:, s % 2, k * D:(k + 1) * D], n_normed)

            pipeline(dve, NG, -2, 2, node_step)

        @block.scalar
        def _(act):
            A = nc.scalar
            act.wait_ge(s_weights, 16 * N_WEIGHTS)
            for raw, high in ((w1, w1_hi), (w2, w2_hi), (whh, whh_hi), (bias, bias_hi)):
                A.activation(high[:], raw[:], ACT.Copy).then_inc(s_split_hi, 1)

            def edge_step(i, m):
                g, s = i + 1, (m + 1) % 2
                if within(g, EG):
                    act.wait_ge(e_turned, g + 1)
                    if due(g - 1):
                        act.wait_ge(e_l1, 4 * (g - 1))
                    for half_ in range(2):
                        A.activation(e_h_hi[:, s, half_, :], bank[half_][:], ACT.Relu).then_inc(e_hhi, 1)
                g, s = i - 1, (m - 1) % 4
                if within(g, EG):
                    act.wait_ge(e_l2, g + 1)
                    if due(g - 3):
                        act.wait_ge(e_stored[s], uses(g - 4, s, 4, 16))
                    A.activation(e_msg[:, s, :, 0:D], bank[6][:].rearrange("p (k d) -> p k d", k=TILES),
                                 ACT.Copy).then_inc(e_msged, 1)
                if within(i, EG):
                    for t in range(TYPES):
                        act.wait_ge(e_l1, 4 * i + t + 1)
                        A.activation(e_r_hi[:, m % 2, t, :], bank[2 + t][:], ACT.Relu).then_inc(e_rhi, 1)

            pipeline(act, EG, -1, 1, edge_step)

            def node_step(i, m):
                g, s = i - 1, (m - 1) % 2
                if within(g, NG):
                    act.wait_ge(n_ued, g + 1)
                    if due(g - 1):
                        act.wait_ge(n_ded, g - 1)
                    A.activation(n_n[:, s, :], n_t[:, s, :], ACT.Tanh, bias=bih[:, 2:3]).then_inc(n_ned, 1)
                g, s = i, m % 2
                if within(g, NG):
                    act.wait_ge(n_gate, 4 * g + 1)
                    if due(g - 1):
                        act.wait_ge(n_ted, g - 1)
                    A.activation(n_r[:, s, :], bank[3][:], ACT.Sigmoid, bias=bsum[:, 0:1]).then_inc(n_red, 1)
                g, s = i + 1, (m + 1) % 2
                if within(g, NG):
                    act.wait_ge(n_turned, g + 1)
                    if due(g - 1):
                        act.wait_ge(n_gate, 4 * (g - 1))
                    A.activation(n_h_hi[:, s, :], bank[s][:], ACT.Relu).then_inc(n_hhi, 1)
                    act.wait_ge(n_summed, g + 1)
                    A.activation(n_agg[:, s, :], bank[2][:], ACT.Copy).then_inc(n_agged, 1)
                g, s = i, m % 2
                if within(g, NG):
                    act.wait_ge(n_gate, 4 * g + 4)
                    if due(g - 1):
                        act.wait_ge(n_eed, g - 1)
                    A.activation(n_zc[:, s, :], bank[6][:], ACT.Sigmoid, bias=bneg[:, 1:2],
                                 scale=-1.0).then_inc(n_zed, 1)

            pipeline(act, NG, -1, 1, node_step)

        @block.tensor
        def _(pe):
            T = nc.tensor

            def product(o, w_hi, w_lo, v_hi, v_lo, start, stop, **kw):
                T.matmul(o, w_hi, v_hi, start=start, stop=False, **kw)
                T.matmul(o, w_hi, v_lo, start=False, stop=False, **kw)
                return T.matmul(o, w_lo, v_hi, start=False, stop=stop, **kw)

            pe.wait_ge(s_onehot_hist, 1)
            T.matmul(bank[7][:, 0:P], high_1h[:, 0:4, :], low_1h[:, 0:4, :], start=True, stop=False)
            with pe.Fori(1, ECOLS // 4 - 1) as c:
                T.matmul(bank[7][:, 0:P], high_1h[:, bass.ds(c * 4, 4), :], low_1h[:, bass.ds(c * 4, 4), :],
                         start=False, stop=False)
            T.matmul(bank[7][:, 0:P], high_1h[:, ECOLS - 4:ECOLS, :], low_1h[:, ECOLS - 4:ECOLS, :],
                     start=False, stop=True).then_inc(s_hist, 1)
            pe.wait_ge(s_const, 1)

            def edge_step(i, m):
                g, s = i + 1, (m + 1) % 2
                if within(g, EG):
                    pe.wait_ge(e_normed, g + 1)
                    if due(2 * g):
                        pe.wait_ge(e_hlo, 2 * g)
                    for k in range(2 * TILES):
                        last = T.transpose(bank[k // TILES][:, (k % TILES) * P:(k % TILES + 1) * P],
                                           e_y[:, s, k, :], ident[:])
                    last.then_inc(e_turned, 1)
                g, s = i - 1, (m - 1) % 2
                if within(g, EG):
                    pe.wait_ge(e_rlo, 4 * (g + 1))
                    if due(g):
                        pe.wait_ge(e_msged, g)
                    for k in range(TILES):
                        o = bank[6][:, k * D:(k + 1) * D]
                        cols = slice(k * P, (k + 1) * P)
                        T.matmul(o, e_onehot[:, (m - 1) % 4, cols], bias2[:], start=True, stop=False)
                        for t in range(TYPES):
                            last = product(o, e_r_hi[:, s, t, cols], e_r_lo[:, s, t, cols],
                                           w2_hi[:, t * D:(t + 1) * D], w2_lo[:, t * D:(t + 1) * D],
                                           False, t == TYPES - 1)
                    last.then_inc(e_l2, 1)
                if within(i, EG):
                    pe.wait_ge(e_hlo, 2 * (i + 1))
                    pe.wait_ge(e_oh, i + 1)
                    for t in range(TYPES):
                        if due(i):
                            pe.wait_ge(e_rlo, 4 * (i - 1) + t + 1)
                        o = bank[2 + t][:]
                        T.matmul(o, bias1[:, t, :], e_onehot[:, m % 4, :], start=True, stop=False)
                        for k in range(2):
                            cols = slice((2 * t + k) * D, (2 * t + k + 1) * D)
                            last = product(o, w1_hi[:, cols], w1_lo[:, cols], e_h_hi[:, m % 2, k, :],
                                           e_h_lo[:, m % 2, k, :], False, k == 1)
                        last.then_inc(e_l1, 1)

            pipeline(pe, EG, -1, 1, edge_step)

            pe.wait_ge(s_hist_ops, 4)
            T.matmul(bank[7][0:BUCKETS, P:P + BUCKETS], same_high[:], hist_before[:], start=True, stop=False)
            T.matmul(bank[7][0:BUCKETS, P:P + BUCKETS], later_high[:], hist_total[:], start=False,
                     stop=True).then_inc(s_start_mm, 1)
            pe.wait_ge(e_msged, EG)
            pe.wait_ge(s_starts_i, 1)

            def gate(b, row, s, sources):
                cols = slice(row * D, (row + 1) * D)
                last = None
                if "h" in sources:
                    last = product(bank[b][:], whh_hi[:, cols], whh_lo[:, cols], n_h_hi[:, s, :], n_h_lo[:, s, :],
                                   True, "a" not in sources)
                if "a" in sources:
                    last = T.matmul(bank[b][:], wih[:, cols], n_agg[:, s, :], start="h" not in sources, stop=True)
                last.then_inc(n_gate, 1)

            def node_step(i, m):
                if within(i, NG):
                    pe.wait_ge(n_hlo, i + 1)
                    pe.wait_ge(n_agged, i + 1)
                    if due(i):
                        pe.wait_ge(n_red, i)
                    gate(3, 0, m % 2, "ha")
                    if due(i):
                        pe.wait_ge(n_ted, i)
                    gate(4, 2, m % 2, "h")
                g, s = i + 1, (m + 1) % 2
                if within(g, NG):
                    pe.wait_ge(n_normed, g + 1)
                    if due(g - 1):
                        pe.wait_ge(n_ded, g - 1)
                    for k in range(TILES):
                        last = T.transpose(bank[s][:, k * P:(k + 1) * P], n_y[:, s, k * D:(k + 1) * D], ident[:])
                    last.then_inc(n_turned, 1)
                    pe.wait_ge(n_seled, g + 1)
                    if due(g):
                        pe.wait_ge(n_agged, g)
                    for k in range(TILES):
                        last = T.matmul(bank[2][:, k * P:(k + 1) * P], n_win[:, (m + 1) % 4, k, 0:D],
                                        n_sel[:, s, k * P:(k + 1) * P], start=True, stop=True)
                    last.then_inc(n_summed, 1)
                if within(i, NG):
                    if due(i):
                        pe.wait_ge(n_ued, i)
                    gate(5, 2, m % 2, "a")
                    if due(i):
                        pe.wait_ge(n_zed, i)
                    gate(6, 1, m % 2, "ha")
                g, s = i - 1, (m - 1) % 2
                if within(g, NG):
                    pe.wait_ge(n_eed, g + 1)
                    if due(g):
                        pe.wait_ge(n_outed, g)
                    for k in range(TILES):
                        last = T.transpose(bank[7][:, k * P:(k + 1) * P], n_e[:, s, k * P:(k + 1) * P], ident[:])
                    last.then_inc(n_back, 1)

            pipeline(pe, NG, -1, 1, node_step)


def kernel(**inputs):
    import numpy as np
    import concourse.bacc as bacc
    from concourse.bass_utils import run_bass_kernel_spmd

    src, dst, types = (np.asarray(inputs[n]) for n in ("src", "dst", "edge_type_4"))
    edges = src.shape[0]
    eg = groups_of(edges)
    padded = np.zeros((3, eg * GROUP), np.int32)
    padded[0, :edges], padded[1, :edges], padded[2, :edges] = src, dst, types
    dst_marked = np.full(eg * GROUP, -1, np.int32)
    dst_marked[:edges] = dst
    arrays = {
        "x": np.ascontiguousarray(inputs["x"]),
        "edge_rows": np.ascontiguousarray(
            padded[0:2].reshape(2, eg, TILES, P).transpose(3, 1, 0, 2).reshape(P, eg, 2 * TILES)),
        "dst_cols": np.ascontiguousarray(dst_marked.reshape(eg * TILES, P).T),
        "types": padded[2:3],
        "W1": np.ascontiguousarray(inputs["L0_gnn_W1"]),
        "b1": np.ascontiguousarray(inputs["L0_gnn_b1"]),
        "W2": np.ascontiguousarray(inputs["L0_gnn_W2"]),
        "b2": np.ascontiguousarray(inputs["L0_gnn_b2"]),
        "WihT": np.ascontiguousarray(np.asarray(inputs["L0_gnn_W_ih"]).T),
        "WhhT": np.ascontiguousarray(np.asarray(inputs["L0_gnn_W_hh"]).T),
        "b_ih": np.ascontiguousarray(np.asarray(inputs["L0_gnn_b_ih"]).reshape(3, D).T),
        "b_hh": np.ascontiguousarray(np.asarray(inputs["L0_gnn_b_hh"]).reshape(3, D).T),
    }
    nc = bacc.Bacc("TRN2", target_bir_lowering=False, num_devices=1)
    args = [nc.dram_tensor(f"in_{name}", a.shape, mybir.dt.from_np(a.dtype), kind="ExternalInput").ap()
            for name, a in arrays.items()]
    out = nc.dram_tensor("out_0", arrays["x"].shape, F32, kind="ExternalOutput").ap()
    gnn_layer(nc, *args, out)
    r = run_bass_kernel_spmd(nc, [{f"in_{name}": a for name, a in arrays.items()}], core_ids=[0])
    return r.results[0]["out_0"]
```

```python
from contextlib import ExitStack

import concourse.bass as bass
from concourse import mybir

F32 = mybir.dt.float32
F32R = mybir.dt.float32r
BF16 = mybir.dt.bfloat16
I32 = mybir.dt.int32
ALU = mybir.AluOpType
ACT = mybir.ActivationFunctionType
AX_X = mybir.AxisListType.X

P = 128
D = 128
TYPES = 4
TILES = 4
GROUP = TILES * P
EPS = 1e-5
BIG = float(2 ** 100)
UNROLL = 4
HEAD = 8
BUCKETS = 32
HIST_UNROLL = 12
HIST_PARTS = 4
PITCH = 144
ROW = D + 1


def groups_of(rows):
    return -(-rows // GROUP)


def due(value):
    return not isinstance(value, int) or value > 0


def within(g, count):
    return not isinstance(g, int) or 0 <= g < count


def uses(g, slot, ring, inc):
    return (g - slot) * (inc // ring) + inc


def pipeline(eng, count, first, last, step):
    end = (count - UNROLL - 1) // UNROLL * UNROLL
    for i in range(first, HEAD):
        step(i, i % UNROLL)
    with eng.Fori(HEAD, end - UNROLL + 1, UNROLL) as i:
        for j in range(UNROLL):
            step(i + j, j)
    for i in range(end, count + last):
        step(i, i % UNROLL)


def gnn_layer(nc, x, edge_rows, dst_cols, dst_flat, types, W1, b1, W2, b2, WihT, WhhT, b_ih, b_hh, out):
    NODES = x.shape[0]
    NG = groups_of(NODES)
    EG = edge_rows.shape[1]
    ECOLS = EG * TILES
    EROWS = ECOLS * P

    DENSE = EROWS
    messages = nc.dram_tensor("messages", (DENSE + NG * GROUP, PITCH), F32, kind="Internal").ap()
    node_sums = nc.dram_tensor("node_sums", (1 + NG * GROUP, D), F32, kind="Internal").ap()
    starts_dram = nc.dram_tensor("starts", (BUCKETS * BUCKETS,), I32, kind="Internal").ap()

    ctx = ExitStack()
    with ctx:
        def sb(name, shape, dt=F32):
            return ctx.enter_context(nc.sbuf_tensor(name, shape, dt))

        def sem(name):
            return ctx.enter_context(nc.semaphore(name))

        iota_i = sb("iota_i", [P, P], I32)
        iota = sb("iota", [P, P])
        part_i = sb("part_i", [P, 3], I32)
        part = sb("part", [P, 3])
        ident = sb("ident", [P, P])
        tile_base_i = sb("tile_base_i", [P, NG * TILES], I32)
        tile_base = sb("tile_base", [P, NG * TILES])
        power = sb("power", [P, 2 * TILES])
        gathers_may_start = sb("gathers_may_start", [1, 1])
        ones128 = sb("ones128", [P, P])
        ones32 = ones128[:, 0:BUCKETS]
        w1_hi = sb("w1_hi", [P, TYPES * 2 * D], F32R)
        w1_lo = sb("w1_lo", [P, TYPES * 2 * D], F32R)
        w2_hi = sb("w2_hi", [P, TYPES * D], F32R)
        w2_lo = sb("w2_lo", [P, TYPES * D], F32R)
        wih = sb("wih", [P, 3 * D])
        whh = sb("whh", [P, 3 * D])
        whh_hi = sb("whh_hi", [P, 3 * D], F32R)
        whh_lo = sb("whh_lo", [P, 3 * D], F32R)
        wih_hi = sb("wih_hi", [P, 3 * D], F32R)
        wih_lo = sb("wih_lo", [P, 3 * D], F32R)
        bih = sb("bih", [P, 3])
        bhh = sb("bhh", [P, 3])
        bsum = sb("bsum", [P, 3])
        bneg = sb("bneg", [P, 3])
        bias = sb("bias", [2 * TYPES, 2, D])
        bias_hi = sb("bias_hi", [2 * TYPES, 2, D], F32R)
        bias_lo = sb("bias_lo", [2 * TYPES, 2, D], F32R)
        bias_parts = sb("bias_parts", [2 * TYPES, 2, D])
        bias1 = sb("bias1", [2 * TYPES, TYPES, D], F32R)
        bias2 = sb("bias2", [2 * TYPES, D], F32R)
        r4_i = sb("r4_i", [2 * TYPES, 1], I32)
        r4 = sb("r4", [2 * TYPES, 1])
        upper = sb("upper", [2 * TYPES, 2])
        pick = sb("pick", [2 * TYPES, TYPES])
        minus_big = sb("minus_big", [2 * TYPES, TYPES])

        dst_i = sb("dst_i", [P, ECOLS], I32)
        dst_f = sb("dst_f", [P, ECOLS])
        q_i = sb("q_i", [P, 2, ECOLS], I32)
        q_f = sb("q_f", [P, 2, ECOLS])
        block_mask = sb("block_mask", [P, 4])
        hist4 = sb("hist4", [P, 4, BUCKETS])
        hist = sb("hist", [P, BUCKETS])
        hist_upto = sb("hist_upto", [P, BUCKETS])
        hist_before = sb("hist_before", [P, BUCKETS])
        hist_total = sb("hist_total", [P, BUCKETS])
        same_high = sb("same_high", [P, BUCKETS])
        later_high = sb("later_high", [P, BUCKETS])
        starts_i = sb("starts_i", [BUCKETS, BUCKETS], I32)
        starts = sb("starts_row", [1, BUCKETS * BUCKETS], I32)
        full = sb("full", [BUCKETS, BUCKETS])
        odd = sb("odd", [P, 2])
        odd_sum = sb("odd_sum", [P, 1])
        general = sb("general", [1, 1], I32)
        g_row = sb("g_row", [P, 1], I32)

        rows_all = sb("rows_all", [P, EG, 2 * TILES], I32)
        rows_now = sb("rows_now", [P, 4, 2 * TILES], I32)
        e_x = sb("e_x", [P, 2, 2 * TILES, D])
        e_h = sb("e_h", [P, 2, 2 * TILES, D])
        e_h_hi = sb("e_h_hi", [P, 2, 2, GROUP], F32R)
        e_h_lo = sb("e_h_lo", [P, 2, 2, GROUP], F32R)
        e_r_hi = sb("e_r_hi", [P, 2, TYPES, GROUP], F32R)
        e_r_lo = sb("e_r_lo", [P, 2, TYPES, GROUP], F32R)
        e_type = sb("e_type", [2 * TYPES, 4, GROUP], I32)
        e_onehot = sb("e_onehot", [2 * TYPES, 4, GROUP], F32R)
        e_msg_t = sb("e_msg_t", [P, 2, GROUP])
        e_msg = sb("e_msg", [P, 4, TILES, ROW])
        raw = e_msg[:].rearrange("p a k d -> p (a k d)")
        w1 = raw[:, 0:TYPES * 2 * D]
        w2 = raw[:, TYPES * 2 * D:TYPES * 3 * D]

        bn = sb("bn", [P, 2 * TILES, 6])
        pair = sb("pair", [P, 2 * TILES, 2])
        diff = sb("diff", [P, 2 * TILES])
        minus_mean = sb("minus_mean", [P, 2, 2 * TILES])
        quarter = sb("quarter", [P, 2 * TILES])
        within_half = sb("within_half", [P, 2 * TILES])
        var = sb("var", [P, 2, 2 * TILES])
        std = sb("std", [P, 2, 2 * TILES])
        rstd = sb("rstd", [P, 2, 2 * TILES])
        shift = sb("shift", [P, 2, 2 * TILES])

        n_all = sb("n_all", [P, ECOLS * BUCKETS])
        taken = [0]

        def carve(ring, width):
            at = taken[0]
            taken[0] += ring * width
            return n_all[:, at:at + ring * width].rearrange("p (r w) -> p r w", r=ring)

        n_x = e_x[:].rearrange("p a (b k) d -> p (a b) (k d)", b=2)
        n_xh = e_h[:].rearrange("p a (b k) d -> p (a b) (k d)", b=2)
        n_h = carve(2, GROUP)
        n_sel = carve(2, GROUP)
        n_r = carve(2, GROUP)
        n_zc = carve(2, GROUP)
        n_t = carve(2, GROUP)
        n_n = carve(2, GROUP)
        n_d = carve(2, GROUP)
        n_e = carve(2, GROUP)
        n_out = carve(4, GROUP)
        n_win = sb("n_win", [P, 4, TILES, ROW])
        n_rel = sb("n_rel", [P, 2, TILES])
        n_h_hi = e_r_hi[:, 0, 0:2, :]
        n_h_lo = e_r_lo[:, 0, 0:2, :]
        n_a_hi = e_r_hi[:, 1, 0:2, :]
        n_a_lo = e_r_lo[:, 1, 0:2, :]
        half = ECOLS * BUCKETS // 2
        high_1h = n_all[:, 0:half].bitcast(BF16).rearrange("p (c b) -> p c b", b=BUCKETS)
        low_1h = n_all[:, half:2 * half].bitcast(BF16).rearrange("p (c b) -> p c b", b=BUCKETS)

        descend = n_all[:, 0:2 * ECOLS].bitcast(I32).rearrange("p (a c) -> p a c", a=2)
        descends = n_all[:, 2 * ECOLS:3 * ECOLS]
        g_all = n_out.rearrange("p r w -> p (r w)")
        g_blank = g_all[:, 0:TILES * PITCH].rearrange("p (k d) -> p k d", k=TILES)
        g_all = g_all[:, TILES * PITCH:]
        g_sum, g_dst, g_same, g_msg = (g_all[:, at:at + PITCH] for at in range(0, 4 * PITCH, PITCH))

        bank = [ctx.enter_context(nc.psum_tensor(f"bank{b}", [P, GROUP], F32)) for b in range(8)]

        s_weights = sem("s_weights")
        s_rows = sem("s_rows")
        s_dst = sem("s_dst")
        s_iota = sem("s_iota")
        s_const = sem("s_const")
        s_power = sem("s_power")
        s_split_hi = sem("s_split_hi")
        s_split = sem("s_split")
        s_prep = sem("s_prep")
        s_onehot_hist = sem("s_onehot_hist")
        s_hist = sem("s_hist")
        s_hist_ops = sem("s_hist_ops")
        s_start_mm = sem("s_start_mm")
        s_starts_i = sem("s_starts_i")
        s_starts_out = sem("s_starts_out")
        s_starts = sem("s_starts")
        s_descend = sem("s_descend")
        s_tiles_seen = sem("s_tiles_seen")
        s_odd_ops = sem("s_odd_ops")
        s_odd = sem("s_odd")
        s_odd_mm = sem("s_odd_mm")
        s_general = sem("s_general")

        g_zeroed = sem("g_zeroed")
        g_blanked = sem("g_blanked")
        g_cleared = sem("g_cleared")
        g_zero_sums = sem("g_zero_sums")
        g_copied = sem("g_copied")
        g_loaded = sem("g_loaded")
        g_spread = sem("g_spread")
        g_across = sem("g_across")
        g_samed = sem("g_samed")
        g_added = sem("g_added")
        g_indexed = sem("g_indexed")
        g_steps = sem("g_steps")
        g_fetched = sem("g_fetched")
        g_summed = sem("g_summed")
        g_scattered = sem("g_scattered")

        e_staged = sem("e_staged")
        e_gated = sem("e_gated")
        e_gathered = [sem(f"e_gathered{s}") for s in range(2)]
        e_typed = [sem(f"e_typed{s}") for s in range(4)]
        e_stored = [sem(f"e_stored{s}") for s in range(4)]
        ln_ops = sem("ln_ops")
        e_var = sem("e_var")
        e_std = sem("e_std")
        e_recip = sem("e_recip")
        e_shift = sem("e_shift")
        e_normed = sem("e_normed")
        e_turned = sem("e_turned")
        e_hhi = sem("e_hhi")
        e_hlo = sem("e_hlo")
        e_oh = sem("e_oh")
        e_l1 = sem("e_l1")
        e_rhi = sem("e_rhi")
        e_rlo = sem("e_rlo")
        e_l2 = sem("e_l2")
        e_msg_ted = sem("e_msg_ted")
        e_back = sem("e_back")
        e_msged = sem("e_msged")
        e_dsted = sem("e_dsted")

        n_loaded = [sem(f"n_loaded{s}") for s in range(4)]
        n_windowed = [sem(f"n_windowed{s}") for s in range(4)]
        n_stored = [sem(f"n_stored{s}") for s in range(4)]
        n_var = sem("n_var")
        n_rstd = sem("n_rstd")
        n_shift = sem("n_shift")
        n_normed = sem("n_normed")
        n_reled = sem("n_reled")
        n_seled = sem("n_seled")
        n_xhed = sem("n_xhed")
        n_turned = sem("n_turned")
        n_summed = sem("n_summed")
        n_hhi = sem("n_hhi")
        n_hlo = sem("n_hlo")
        n_ahi = sem("n_ahi")
        n_alo = sem("n_alo")
        n_gate = sem("n_gate")
        n_red = sem("n_red")
        n_zed = sem("n_zed")
        n_ted = sem("n_ted")
        n_ued = sem("n_ued")
        n_ned = sem("n_ned")
        n_ded = sem("n_ded")
        n_eed = sem("n_eed")
        n_back = sem("n_back")
        n_outed = sem("n_outed")

        N_WEIGHTS = 10
        N_SPLITS = 5
        LN_STEPS = 3
        block = ctx.enter_context(nc.Block())

        @block.sync
        def _(sp):
            sp.dma_start(rows_all[:], edge_rows).then_inc(s_rows, 16)
            sp.dma_start(dst_i[:], dst_cols).then_inc(s_dst, 16)
            sp.dma_start(w1.rearrange("p (t k o) -> p t k o", t=TYPES, k=2),
                         W1.rearrange("t (k p) o -> p t k o", p=P)).then_inc(s_weights, 16)
            sp.dma_start(w2.rearrange("p (t o) -> p t o", t=TYPES),
                         W2.rearrange("t p o -> p t o")).then_inc(s_weights, 16)
            sp.dma_start(wih[:], WihT).then_inc(s_weights, 16)
            sp.dma_start(whh[:], WhhT).then_inc(s_weights, 16)
            sp.dma_start(bih[:], b_ih).then_inc(s_weights, 16)
            sp.dma_start(bhh[:], b_hh).then_inc(s_weights, 16)
            for copy in range(2):
                sp.dma_start(bias[copy * TYPES:(copy + 1) * TYPES, 0, :], b1).then_inc(s_weights, 16)
                sp.dma_start(bias[copy * TYPES:(copy + 1) * TYPES, 1, :], b2).then_inc(s_weights, 16)

            def edge_io(i, m):
                g, s = i + 2, (m + 2) % 4
                if within(g, EG):
                    if due(g - 3):
                        sp.wait_ge(e_oh, g - 3)
                    sp.dma_start(e_type[:, s, :], types[:, bass.ds(g * GROUP, GROUP)]
                                 .to_broadcast([2 * TYPES, GROUP])).then_inc(e_typed[s], 16)
                g, s = i - 3, (m - 3) % 4
                if within(g, EG):
                    sp.wait_ge(e_msged, g + 1)
                    sp.wait_ge(e_dsted, g + 1)
                    sp.dma_start(messages[bass.ds(g * GROUP, GROUP), 0:ROW].rearrange("(k p) d -> p k d", p=P),
                                 e_msg[:, s]).then_inc(e_stored[s], 16)
                if isinstance(i, int) and i == 5:
                    sp.wait_ge(s_hist, 1)
                    for n in range(2):
                        sp.dma_start(descend[:, n, :], dst_flat[n:n + EROWS].rearrange("(p c) -> p c", p=P)
                                     ).then_inc(s_descend, 16)
                if isinstance(i, int) and i == 7:
                    sp.wait_ge(s_starts_i, 1)
                    sp.dma_start(starts_dram.rearrange("(h l) -> h l", l=BUCKETS), starts_i[:]
                                 ).then_inc(s_starts_out, 16)
                    sp.wait_ge(s_starts_out, 16)
                    sp.dma_start(starts[:], starts_dram.rearrange("(a n) -> a n", a=1)).then_inc(s_starts, 16)

            pipeline(sp, EG, -2, 3, edge_io)
            for s in range(4):
                sp.wait_ge(e_stored[s], uses((EG - 1 - s) // 4 * 4 + s, s, 4, 16))
            sp.wait_ge(s_starts, 16)

            sp.wait_ge(s_general, 1)
            with sp.If(sp.value_load(general[:], min_val=0, max_val=1) > 0):
                with sp.Fori(0, NG) as g:
                    sp.wait_ge(g_blanked, g + 1)
                    sp.dma_start(messages[bass.ds(g * GROUP + DENSE, GROUP), 0:ROW].rearrange("(k p) d -> p k d", p=P),
                                 g_blank[:, :, 0:ROW]).then_inc(g_cleared, 16)
                    sp.dma_start(node_sums[bass.ds(g * GROUP + 1, GROUP), :].rearrange("(k p) d -> p k d", p=P),
                                 g_blank[:, :, 0:D]).then_inc(g_zero_sums, 16)
                sp.dma_start(node_sums[0:1, :], g_blank[0:1, 0, 0:D]).then_inc(g_zero_sums, 16)
                with sp.Fori(0, ECOLS) as c:
                    sp.wait_ge(g_summed, c + 1)
                    sp.dma_start(g_msg[:, 0:ROW], messages[bass.ds(c * P, P), 0:ROW]).then_inc(g_loaded, 16)
                sp.wait_ge(g_steps, 3 * ECOLS + 1)
                with sp.Fori(0, NG) as g:
                    sp.dma_start(messages[bass.ds(g * GROUP + DENSE, GROUP), 0:D],
                                 node_sums[bass.ds(g * GROUP + 1, GROUP), :]).then_inc(g_copied, 16)
                sp.wait_ge(g_cleared, 16 * NG)
                sp.wait_ge(g_copied, 16 * NG)

            TAIL = NODES - (NG - 1) * GROUP
            parts = [(k, min(P, TAIL - k * P)) for k in range(TILES) if TAIL > k * P]

            def node_io(i, m):
                g, s = i + 4, m % 4
                if within(g, NG):
                    if due(g - 3):
                        sp.wait_ge(n_xhed, g - 3)
                    if isinstance(g, int) and g == NG - 1:
                        for k, rows in parts:
                            sp.dma_start(n_x[0:rows, s, k * D:(k + 1) * D],
                                         x[g * GROUP + k * P:g * GROUP + k * P + rows, :]).then_inc(n_loaded[s], 16)
                    else:
                        sp.dma_start(n_x[:, s, :].rearrange("p (k d) -> p k d", k=TILES),
                                     x[bass.ds(g * GROUP, GROUP), :].rearrange("(k p) d -> p k d", p=P)
                                     ).then_inc(n_loaded[s], 16)
                    if due(g - 3):
                        sp.wait_ge(n_summed, g - 3)
                    for k in range(TILES):
                        start = sp.value_load(starts[0:1, bass.ds(g * TILES + k, 1)],
                                              min_val=0, max_val=DENSE + NG * GROUP - P)
                        sp.dma_start(n_win[:, s, k, :], messages[bass.ds(start, P), 0:ROW]
                                     ).then_inc(n_windowed[s], 16)
                g, s = i - 2, (m - 2) % 4
                if within(g, NG):
                    sp.wait_ge(n_outed, g + 1)
                    if isinstance(g, int) and g == NG - 1:
                        for k, rows in parts:
                            sp.dma_start(out[g * GROUP + k * P:g * GROUP + k * P + rows, :],
                                         n_out[0:rows, s, k * D:(k + 1) * D]).then_inc(n_stored[s], 16)
                    else:
                        sp.dma_start(out[bass.ds(g * GROUP, GROUP), :].rearrange("(k p) d -> p k d", p=P),
                                     n_out[:, s, :].rearrange("p (k d) -> p k d", k=TILES)
                                     ).then_inc(n_stored[s], 16)

            pipeline(sp, NG, -4, 2, node_io)
            for s in range(4):
                last = (NG - 1 - s) // 4 * 4 + s
                extra = 16 * (len(parts) - 1) if last == NG - 1 else 0
                sp.wait_ge(n_stored[s], uses(last, s, 4, 16) + extra)

        @block.gpsimd
        def _(pool):
            nc.gpsimd.iota(iota_i[:], pattern=[[1, P]], base=0, channel_multiplier=0)
            nc.gpsimd.iota(tile_base_i[:], pattern=[[P, NG * TILES]], base=0, channel_multiplier=0)
            nc.gpsimd.iota(part_i[:, 0:1], pattern=[[0, 1]], base=0, channel_multiplier=1).then_inc(s_iota, 1)

            nc.gpsimd.memset(power[:], -0.5).then_inc(s_power, 1)
            pool.wait_ge(s_power, 1)

            def stage(g, s):
                nc.gpsimd.tensor_copy(rows_now[:, s, :], rows_all[:, bass.ds(g, 1), :]
                                      .rearrange("p a k -> p (a k)")).then_inc(e_staged, 1)

            pool.wait_ge(s_rows, 16)
            stage(0, 0)

            def gather(g, m):
                if within(g + 1, EG):
                    stage(g + 1, (m + 1) % 4)
                pool.wait_ge(e_staged, g + 1)
                if due(g):
                    pool.wait_ge(e_gated, g)
                if due(g - 1):
                    pool.wait_ge(e_normed, g - 1)
                nc.gpsimd.tensor_tensor(gathers_may_start[:], power[0:1, 0:1], power[0:1, 0:1],
                                        ALU.add).then_inc(e_gated, 1)
                for k in range(2 * TILES):
                    nc.gpsimd.indirect_dma_start(
                        e_x[:, m % 2, k, :], None, x,
                        bass.IndirectOffsetOnAxis(ap=rows_now[:, m % 4, k:k + 1], axis=0)
                    ).then_inc(e_gathered[m % 2], 16)

            pipeline(pool, EG, 0, 0, gather)

            pool.wait_ge(s_general, 1)
            with pool.If(pool.value_load(general[:], min_val=0, max_val=1) > 0):

                def step(value=None):
                    if value is not None:
                        pool.wait_ge(g_steps, value)
                    nc.gpsimd.tensor_tensor(gathers_may_start[:], power[0:1, 0:1], power[0:1, 0:1],
                                            ALU.add).then_inc(g_steps, 1)

                pool.wait_ge(g_zero_sums, 16 * (NG + 1))
                pool.wait_ge(e_gated, EG)
                step()
                with pool.Fori(0, ECOLS) as c:
                    pool.wait_ge(g_indexed, c + 1)
                    step(3 * c + 1)
                    nc.gpsimd.indirect_dma_start(g_sum[:, 0:D], None, node_sums,
                                                 bass.IndirectOffsetOnAxis(ap=g_row[:], axis=0)).then_inc(g_fetched, 16)
                    pool.wait_ge(g_summed, c + 2)
                    step(3 * c + 2)
                    nc.gpsimd.indirect_dma_start(node_sums, bass.IndirectOffsetOnAxis(ap=g_row[:], axis=0),
                                                 g_sum[:, 0:D], None).then_inc(g_scattered, 16)
                    pool.wait_ge(g_scattered, 16 * c + 16)
                    step(3 * c + 3)

            def node_side(i, m):
                g, s = i - 1, (m - 1) % 2
                if within(g, NG):
                    pool.wait_ge(n_ded, g + 1)
                    pool.wait_ge(n_zed, g + 1)
                    if due(g - 1):
                        pool.wait_ge(n_back, g - 1)
                    nc.gpsimd.tensor_tensor(n_e[:, s, :], n_d[:, s, :], n_zc[:, s, :], ALU.mult).then_inc(n_eed, 1)
                g, s = i + 2, (m + 2) % 4
                if within(g, NG):
                    pool.wait_ge(n_var, g + 1)
                    if due(g - 1):
                        pool.wait_ge(n_normed, g - 1)
                    nc.gpsimd.tensor_tensor(rstd[:, s % 2, 0:TILES], var[:, s % 2, 0:TILES], power[:, 0:TILES],
                                            ALU.pow).then_inc(n_rstd, 1)
                    pool.wait_ge(n_rstd, g + 1)
                    nc.gpsimd.tensor_tensor(shift[:, s % 2, 0:TILES], minus_mean[:, s % 2, 0:TILES],
                                            rstd[:, s % 2, 0:TILES], ALU.mult).then_inc(n_shift, 1)
                g, s = i + 3, (m + 3) % 4
                if within(g, NG):
                    pool.wait_ge(n_windowed[s], uses(g, s, 4, 64))
                    if due(g - 1):
                        pool.wait_ge(n_seled, g - 1)
                    nc.gpsimd.tensor_tensor(
                        n_rel[:, s % 2, :], n_win[:, s, :, D:ROW].rearrange("p k a -> p (k a)"),
                        tile_base[:, bass.ds(g * TILES, TILES)], ALU.subtract).then_inc(n_reled, 1)
                g, s = i + 1, (m + 1) % 4
                if within(g, NG):
                    pool.wait_ge(n_normed, g + 1)
                    if due(g - 3):
                        pool.wait_ge(n_outed, g - 3)
                    nc.gpsimd.tensor_tensor(n_xh[:, s, :], n_h[:, s % 2, :], n_x[:, s, :], ALU.add).then_inc(n_xhed, 1)

            pipeline(pool, NG, -3, 1, node_side)

        @block.vector
        def _(dve):
            chain = [0]

            def link(ins):
                chain[0] += 1
                ins.then_inc(s_prep, 1)
                dve.wait_ge(s_prep, chain[0])

            V = nc.vector
            dve.wait_ge(s_iota, 1)
            V.tensor_copy(iota[:], iota_i[:])
            V.tensor_copy(tile_base[:], tile_base_i[:])
            V.tensor_scalar(part_i[:, 1:2], part_i[:, 0:1], 5, None, ALU.arith_shift_right)
            V.memset(ones128[:], 1.0)
            V.tensor_scalar(r4_i[:], part_i[0:2 * TYPES, 0:1], TYPES - 1, None, ALU.bitwise_and)
            link(V.tensor_scalar(part_i[:, 2:3], part_i[:, 0:1], BUCKETS - 1, None, ALU.bitwise_and))
            V.tensor_copy(r4[:], r4_i[:])
            link(V.tensor_copy(part[:], part_i[:]))
            V.tensor_scalar(block_mask[:], iota[:, 0:4], part[:, 1:2], None, ALU.is_equal)
            V.tensor_scalar(same_high[:], iota[:, 0:BUCKETS], part[:, 2:3], None, ALU.is_equal)
            V.tensor_scalar(later_high[:], iota[:, 0:BUCKETS], part[:, 2:3], None, ALU.is_gt)
            V.tensor_scalar(pick[:], iota[0:2 * TYPES, 0:TYPES], r4[:], None, ALU.is_equal)
            V.tensor_scalar(upper[:, 0:1], part[0:2 * TYPES, 0:1], float(TYPES), None, ALU.is_lt)
            V.tensor_scalar(upper[:, 1:2], part[0:2 * TYPES, 0:1], float(TYPES), None, ALU.is_ge)
            link(V.tensor_scalar(ident[:], iota[:], part[:, 0:1], None, ALU.is_equal))
            link(V.tensor_scalar(minus_big[:], pick[:], BIG, -BIG, ALU.mult, ALU.add))
            link(V.tensor_scalar(minus_big[:], minus_big[:], upper[:, 0:1], None, ALU.mult))
            dve.wait_ge(s_weights, 16 * N_WEIGHTS)
            dve.wait_ge(s_split_hi, N_SPLITS)
            V.tensor_tensor(w1_lo[:], w1, w1_hi[:].bitcast(F32), ALU.subtract)
            V.tensor_tensor(w2_lo[:], w2, w2_hi[:].bitcast(F32), ALU.subtract)
            V.tensor_tensor(whh_lo[:], whh[:], whh_hi[:].bitcast(F32), ALU.subtract)
            V.tensor_tensor(wih_lo[:], wih[:], wih_hi[:].bitcast(F32), ALU.subtract)
            link(V.tensor_tensor(bias_lo[:], bias[:], bias_hi[:].bitcast(F32), ALU.subtract))
            link(V.tensor_scalar(bias_parts[:], bias_hi[:].bitcast(F32), upper[:, 0:1], None, ALU.mult))
            link(V.scalar_tensor_tensor(out=bias_parts[:], in0=bias_lo[:].bitcast(F32), scalar=upper[:, 1:2],
                                        in1=bias_parts[:], op0=ALU.mult, op1=ALU.add))
            V.tensor_copy(bias2[:], bias_parts[:, 1, :])
            for t in range(TYPES):
                V.tensor_scalar(bias1[:, t, :], bias_parts[:, 0, :], pick[:, t:t + 1], minus_big[:, t:t + 1],
                                ALU.mult, ALU.add)
            link(V.tensor_tensor(bsum[:], bih[:], bhh[:], ALU.add))
            V.tensor_scalar(bneg[:], bsum[:], -1.0, None, ALU.mult).then_inc(s_const, 1)

            V.memset(odd[:], 0.0)
            dve.wait_ge(s_dst, 16)
            V.tensor_copy(dst_f[:], dst_i[:])
            V.tensor_scalar(q_i[:, 0, :], dst_i[:], 12, None, ALU.arith_shift_right)
            link(V.tensor_scalar(q_i[:, 1, :], dst_i[:], 7, BUCKETS - 1, ALU.arith_shift_right, ALU.bitwise_and))
            link(V.tensor_copy(q_f[:], q_i[:]))
            done = [0]

            def hist_link(ins):
                done[0] += 1
                ins.then_inc(s_hist_ops, 1)
                dve.wait_ge(s_hist_ops, done[0])

            def count_tiles(i):
                if 0 <= i < HIST_PARTS:
                    cols = slice(i * ECOLS // HIST_PARTS, (i + 1) * ECOLS // HIST_PARTS)
                    n = cols.stop - cols.start
                    for part_, onehot in enumerate((high_1h, low_1h)):
                        last = V.tensor_tensor(onehot[:, cols, :],
                                               iota[:, 0:BUCKETS].unsqueeze(1).to_broadcast([P, n, BUCKETS]),
                                               q_f[:, part_, cols].unsqueeze(2).to_broadcast([P, n, BUCKETS]),
                                               ALU.is_equal)
                    last.then_inc(s_onehot_hist, 1)
                if i == 5:
                    dve.wait_ge(s_hist, 1)
                    hist_link(V.tensor_tensor(hist4[:], bank[7][:, 0:P].rearrange("p (j l) -> p j l", j=4),
                                              block_mask[:].unsqueeze(2).to_broadcast([P, 4, BUCKETS]), ALU.mult))
                    hist_link(V.tensor_reduce(hist[:], hist4[:].rearrange("p j l -> p l j"), AX_X, ALU.add))
                    hist_link(V.tensor_tensor_scan(hist_upto[:], ones32, hist[:], 0.0, ALU.mult, ALU.add))
                    V.tensor_tensor(hist_before[:], hist_upto[:], hist[:], ALU.subtract)
                    hist_link(V.tensor_scalar(hist_total[:], ones32, hist_upto[:, BUCKETS - 1:BUCKETS], None,
                                              ALU.mult))
                if i == 6:
                    dve.wait_ge(s_start_mm, 1)
                    V.tensor_copy(starts_i[:], bank[7][0:BUCKETS, 0:BUCKETS]).then_inc(s_starts_i, 1)
                    V.tensor_scalar(full[:], bank[7][0:BUCKETS, BUCKETS:2 * BUCKETS], float(P), None,
                                    ALU.is_gt).then_inc(s_tiles_seen, 1)
                    dve.wait_ge(s_descend, 32)
                    V.tensor_tensor(descends, descend[:, 0, :], descend[:, 1, :], ALU.is_gt).then_inc(s_odd_ops, 1)
                    dve.wait_ge(s_tiles_seen, 1)
                    V.tensor_reduce(odd[0:BUCKETS, 1:2], full[:], AX_X, ALU.add)
                    dve.wait_ge(s_odd_ops, 1)
                    V.tensor_reduce(odd[:, 0:1], descends, AX_X, ALU.add).then_inc(s_odd_ops, 1)
                    dve.wait_ge(s_odd_ops, 2)
                    V.tensor_reduce(odd_sum[:], odd[:], AX_X, ALU.add).then_inc(s_odd, 1)
                if i == 7:
                    dve.wait_ge(s_odd_mm, 1)
                    V.tensor_scalar(general[:], bank[7][0:1, 0:1], 1.5, None, ALU.is_gt).then_inc(s_general, 1)

            def ln_rows(count, tile):
                for k in range(count):
                    last = V.bn_stats(bn[:, k, :], tile(k))
                last.then_inc(ln_ops, 1)

            def ln_stats(count, slot, base, finish):
                done = [base + 1]
                dve.wait_ge(ln_ops, done[0])

                def ln_link(ins):
                    done[0] = done[0] + 1
                    ins.then_inc(ln_ops, 1)
                    dve.wait_ge(ln_ops, done[0])

                halves = bn[:, 0:count, :].rearrange("p k (h c) -> p k h c", h=2)
                V.tensor_tensor(pair[:, 0:count, :], halves[:, :, 0, 1:3], halves[:, :, 1, 1:3], ALU.add)
                ln_link(V.tensor_tensor(diff[:, 0:count], bn[:, 0:count, 1], bn[:, 0:count, 4], ALU.subtract))
                V.tensor_scalar(minus_mean[:, slot, 0:count], pair[:, 0:count, 0], -0.5, None, ALU.mult)
                V.tensor_scalar(within_half[:, 0:count], pair[:, 0:count, 1], 1.0 / D, EPS, ALU.mult, ALU.add)
                ln_link(V.scalar_tensor_tensor(out=quarter[:, 0:count], in0=diff[:, 0:count], scalar=0.25,
                                               in1=diff[:, 0:count], op0=ALU.mult, op1=ALU.mult))
                V.tensor_tensor(var[:, slot, 0:count], within_half[:, 0:count], quarter[:, 0:count],
                                ALU.add).then_inc(finish, 1)

            def low_hidden(i, m, t):
                dve.wait_ge(e_rhi, 4 * i + t + 1)
                if t == 0 and due(i - 1):
                    dve.wait_ge(e_l2, i - 1)
                V.scalar_tensor_tensor(out=e_r_lo[:, m % 2, t, :], in0=bank[2 + t][:], scalar=0.0,
                                       in1=e_r_hi[:, m % 2, t, :].bitcast(F32), op0=ALU.max,
                                       op1=ALU.subtract).then_inc(e_rlo, 1)

            def edge_step(i, m):
                g, s = i - 1, (m - 1) % 4
                if within(g, EG):
                    if due(g - 3):
                        dve.wait_ge(e_stored[s], uses(g - 4, s, 4, 16))
                    V.tensor_copy(e_msg[:, s, :, D:ROW].rearrange("p k a -> p (k a)"),
                                  dst_f[:, bass.ds(g * TILES, TILES)]).then_inc(e_dsted, 1)
                g, s = i + 1, (m + 1) % 4
                if within(g, EG):
                    dve.wait_ge(e_typed[s], uses(g, s, 4, 16))
                    if due(g - 3):
                        dve.wait_ge(e_l2, g - 3)
                    V.tensor_scalar(e_onehot[:, s, :], e_type[:, s, :], r4[:], None, ALU.is_equal).then_inc(e_oh, 1)
                g, s = i + 2, (m + 2) % 2
                if within(g, EG):
                    dve.wait_ge(e_gathered[s], uses(g, s, 2, 16 * 2 * TILES))
                    ln_rows(2 * TILES, lambda k: e_x[:, s, k, :])
                    ln_stats(2 * TILES, s, g * LN_STEPS, e_var)
                if within(i, EG):
                    for t in range(3):
                        low_hidden(i, m, t)
                if within(g, EG):
                    dve.wait_ge(e_std, g + 1)
                    if due(g - 1):
                        dve.wait_ge(e_normed, g - 1)
                    V.reciprocal(rstd[:, s, :], std[:, s, :]).then_inc(e_recip, 1)
                    dve.wait_ge(e_recip, g + 1)
                    V.tensor_tensor(shift[:, s, :], minus_mean[:, s, :], rstd[:, s, :], ALU.mult).then_inc(e_shift, 1)
                if within(i, EG):
                    low_hidden(i, m, 3)
                g, s = i + 1, (m + 1) % 2
                if within(g, EG):
                    for half_ in range(2):
                        dve.wait_ge(e_hhi, 2 * g + half_ + 1)
                        if half_ == 0 and due(g - 1):
                            dve.wait_ge(e_l1, 4 * (g - 1))
                        V.tensor_tensor(e_h_lo[:, s, half_, :], bank[half_][:],
                                        e_h_hi[:, s, half_, :].bitcast(F32), ALU.subtract).then_inc(e_hlo, 1)
                if isinstance(i, int):
                    count_tiles(i)

            pipeline(dve, EG, -2, 1, edge_step)

            dve.wait_ge(s_general, 1)
            with dve.If(dve.value_load(general[:], min_val=0, max_val=1) > 0):
                dve.wait_ge(s_starts, 16)
                V.tensor_scalar(starts[0:1, 0:NG * TILES], tile_base_i[0:1, :], DENSE, None,
                                ALU.add).then_inc(g_summed, 1)
                V.memset(g_blank, 0.0).then_inc(g_zeroed, 1)
                dve.wait_ge(g_zeroed, 1)
                V.tensor_scalar(g_blank[:, :, D], tile_base[:, 0:TILES], part[:, 0:1], None,
                                ALU.add).then_inc(g_blanked, 1)
                with dve.Fori(1, NG) as g:
                    dve.wait_ge(g_cleared, 16 * g)
                    V.tensor_scalar(g_blank[:, :, D], tile_base[:, bass.ds(g * TILES, TILES)], part[:, 0:1], None,
                                    ALU.add).then_inc(g_blanked, 1)
                with dve.Fori(0, ECOLS) as c:
                    dve.wait_ge(g_loaded, 16 * c + 16)
                    dve.wait_ge(g_steps, 3 * c + 1)
                    V.tensor_scalar(g_row[:], g_msg[:, D:ROW], 1.0, None, ALU.add).then_inc(g_indexed, 1)
                    V.tensor_scalar(g_dst[:, 0:P], ones128[:], g_msg[:, D:ROW], None, ALU.mult).then_inc(g_spread, 1)
                    dve.wait_ge(g_across, c + 1)
                    V.tensor_scalar(g_same[:, 0:P], bank[6][:, 0:P], g_msg[:, D:ROW], None,
                                    ALU.is_equal).then_inc(g_samed, 1)
                    dve.wait_ge(g_added, c + 1)
                    dve.wait_ge(g_fetched, 16 * c + 16)
                    V.tensor_tensor(g_sum[:, 0:D], g_sum[:, 0:D], bank[7][:, 0:D], ALU.add).then_inc(g_summed, 1)

            def node_step(i, m):
                g, s = i, m % 2
                if within(g, NG):
                    dve.wait_ge(n_red, g + 1)
                    dve.wait_ge(n_gate, 4 * g + 2)
                    if due(g - 1):
                        dve.wait_ge(n_ned, g - 1)
                    V.scalar_tensor_tensor(out=n_t[:, s, :], in0=bank[4][:], scalar=bhh[:, 2:3], in1=n_r[:, s, :],
                                           op0=ALU.add, op1=ALU.mult).then_inc(n_ted, 1)
                g, s = i + 2, (m + 2) % 2
                if within(g, NG):
                    dve.wait_ge(n_reled, g + 1)
                    if due(g - 1):
                        dve.wait_ge(n_summed, g - 1)
                    V.tensor_tensor(n_sel[:, s, :].rearrange("p (k n) -> p k n", k=TILES),
                                    iota[:].unsqueeze(1).to_broadcast([P, TILES, P]),
                                    n_rel[:, s, :].unsqueeze(2).to_broadcast([P, TILES, P]),
                                    ALU.is_equal).then_inc(n_seled, 1)
                g, s = i + 1, (m + 1) % 2
                if within(g, NG):
                    dve.wait_ge(n_hhi, g + 1)
                    if due(g - 1):
                        dve.wait_ge(n_gate, 4 * (g - 1))
                    V.tensor_tensor(n_h_lo[:, s, :], bank[s][:], n_h_hi[:, s, :].bitcast(F32),
                                    ALU.subtract).then_inc(n_hlo, 1)
                    dve.wait_ge(n_ahi, g + 1)
                    V.tensor_tensor(n_a_lo[:, s, :], bank[2][:], n_a_hi[:, s, :].bitcast(F32),
                                    ALU.subtract).then_inc(n_alo, 1)
                g, s = i, m % 2
                if within(g, NG):
                    dve.wait_ge(n_gate, 4 * g + 3)
                    dve.wait_ge(n_ted, g + 1)
                    V.tensor_tensor(n_t[:, s, :], bank[5][:], n_t[:, s, :], ALU.add).then_inc(n_ued, 1)
                g, s = i + 3, (m + 3) % 4
                if within(g, NG):
                    tail = isinstance(g, int) and g == NG - 1
                    dve.wait_ge(n_loaded[s], uses(g, s, 4, 16) + (16 * (-(-(NODES - g * GROUP) // P) - 1) if tail else 0))
                    ln_rows(TILES, lambda k: n_x[:, s, k * D:(k + 1) * D])
                g, s = i, m % 2
                if within(g, NG):
                    dve.wait_ge(n_ned, g + 1)
                    if due(g - 1):
                        dve.wait_ge(n_eed, g - 1)
                    V.tensor_tensor(n_d[:, s, :], bank[s][:], n_n[:, s, :], ALU.subtract).then_inc(n_ded, 1)
                g, s = i + 3, (m + 3) % 2
                if within(g, NG):
                    if due(g - 1):
                        dve.wait_ge(n_shift, g - 1)
                    ln_stats(TILES, s, EG * LN_STEPS + g * LN_STEPS, n_var)
                g, s = i - 1, (m - 1) % 4
                if within(g, NG):
                    dve.wait_ge(n_back, g + 1)
                    if due(g - 3):
                        dve.wait_ge(n_stored[s], uses(g - 4, s, 4, 16))
                    V.tensor_tensor(n_out[:, s, :], n_xh[:, s, :], bank[7][:], ALU.subtract).then_inc(n_outed, 1)

            pipeline(dve, NG, -3, 1, node_step)

        @block.scalar
        def _(act):
            A = nc.scalar
            act.wait_ge(s_weights, 16 * N_WEIGHTS)
            for full, high in ((w1, w1_hi), (w2, w2_hi), (whh[:], whh_hi), (wih[:], wih_hi), (bias[:], bias_hi)):
                A.activation(high[:], full, ACT.Copy).then_inc(s_split_hi, 1)

            def high_hidden(i, m, t):
                act.wait_ge(e_l1, 4 * i + t + 1)
                A.activation(e_r_hi[:, m % 2, t, :], bank[2 + t][:], ACT.Relu).then_inc(e_rhi, 1)

            def normalise_edges(g, s, tiles):
                if not within(g, EG):
                    return
                if 0 in tiles:
                    act.wait_ge(e_shift, g + 1)
                    if due(g - 1):
                        act.wait_ge(e_turned, g - 1)
                for k in tiles:
                    last = A.activation(e_h[:, s, k, :], e_x[:, s, k, :], ACT.Relu, scale=rstd[:, s, k:k + 1],
                                        bias=shift[:, s, k:k + 1])
                if 2 * TILES - 1 in tiles:
                    last.then_inc(e_normed, 1)

            def edge_step(i, m):
                g, s = i - 2, (m - 2) % 4
                if within(g, EG):
                    act.wait_ge(e_back, g + 1)
                    if due(g - 3):
                        act.wait_ge(e_stored[s], uses(g - 4, s, 4, 16))
                    A.activation(e_msg[:, s, :, 0:D], bank[7][:].rearrange("p (k d) -> p k d", k=TILES),
                                 ACT.Copy).then_inc(e_msged, 1)
                normalise_edges(i + 1, (m + 1) % 2, (0, 1, 2, 3, 4))
                g, s = i - 1, (m - 1) % 2
                if within(g, EG):
                    act.wait_ge(e_l2, g + 1)
                    A.activation(e_msg_t[:, s, :], bank[6][:], ACT.Copy).then_inc(e_msg_ted, 1)
                normalise_edges(i + 1, (m + 1) % 2, (5, 6, 7))
                if within(i, EG):
                    high_hidden(i, m, 0)
                    high_hidden(i, m, 1)
                g, s = i + 2, (m + 2) % 2
                if within(g, EG):
                    act.wait_ge(e_var, g + 1)
                    A.activation(std[:, s, :], var[:, s, :], ACT.Sqrt).then_inc(e_std, 1)
                if within(i, EG):
                    high_hidden(i, m, 2)
                    high_hidden(i, m, 3)
                g, s = i + 1, (m + 1) % 2
                if within(g, EG):
                    act.wait_ge(e_turned, g + 1)
                    for half_ in range(2):
                        A.activation(e_h_hi[:, s, half_, :], bank[half_][:], ACT.Copy).then_inc(e_hhi, 1)

            pipeline(act, EG, -2, 2, edge_step)

            def normalise(i, m, tiles):
                g, s = i, m % 4
                if not within(g, NG):
                    return
                if 0 in tiles:
                    act.wait_ge(n_shift, g + 1)
                    if due(g - 1):
                        act.wait_ge(n_turned, g - 1)
                        act.wait_ge(n_xhed, g - 1)
                for k in tiles:
                    cols = slice(k * D, (k + 1) * D)
                    last = A.activation(n_h[:, s % 2, cols], n_x[:, s, cols], ACT.Relu,
                                        scale=rstd[:, s % 2, k:k + 1], bias=shift[:, s % 2, k:k + 1])
                if TILES - 1 in tiles:
                    last.then_inc(n_normed, 1)

            def node_step(i, m):
                normalise(i + 1, m + 1, (3,))
                g, s = i, m % 2
                if within(g, NG):
                    act.wait_ge(n_gate, 4 * g + 1)
                    if due(g - 1):
                        act.wait_ge(n_ted, g - 1)
                    A.activation(n_r[:, s, :], bank[3][:], ACT.Sigmoid, bias=bsum[:, 0:1]).then_inc(n_red, 1)
                g, s = i + 1, (m + 1) % 2
                if within(g, NG):
                    act.wait_ge(n_turned, g + 1)
                    if due(g - 1):
                        act.wait_ge(n_gate, 4 * (g - 1))
                    A.activation(n_h_hi[:, s, :], bank[s][:], ACT.Copy).then_inc(n_hhi, 1)
                    act.wait_ge(n_summed, g + 1)
                    A.activation(n_a_hi[:, s, :], bank[2][:], ACT.Copy).then_inc(n_ahi, 1)
                normalise(i + 2, m + 2, (0, 1, 2))
                g, s = i, m % 2
                if within(g, NG):
                    act.wait_ge(n_ued, g + 1)
                    if due(g - 1):
                        act.wait_ge(n_ded, g - 1)
                    A.activation(n_n[:, s, :], n_t[:, s, :], ACT.Tanh, bias=bih[:, 2:3]).then_inc(n_ned, 1)
                    act.wait_ge(n_gate, 4 * g + 4)
                    if due(g - 1):
                        act.wait_ge(n_eed, g - 1)
                    A.activation(n_zc[:, s, :], bank[6][:], ACT.Sigmoid, bias=bneg[:, 1:2],
                                 scale=-1.0).then_inc(n_zed, 1)

            pipeline(act, NG, -2, 1, node_step)

        @block.tensor
        def _(pe):
            T = nc.tensor

            def product(o, w_hi, w_lo, v_hi, v_lo, start, stop, **kw):
                T.matmul(o, w_hi, v_hi, start=start, stop=False, **kw)
                T.matmul(o, w_hi, v_lo, start=False, stop=False, **kw)
                return T.matmul(o, w_lo, v_hi, start=False, stop=stop, **kw)

            def count_tiles(i):
                if i == 5:
                    pe.wait_ge(s_onehot_hist, HIST_PARTS)
                    pe.wait_ge(e_msged, i - 1)
                    T.matmul(bank[7][:, 0:P], high_1h[:, 0:4, :], low_1h[:, 0:4, :], start=True, stop=False)
                    with pe.Fori(1, ECOLS // 4 - HIST_UNROLL, HIST_UNROLL) as c:
                        for n in range(HIST_UNROLL):
                            cols = bass.ds(c * 4 + n * 4, 4)
                            T.matmul(bank[7][:, 0:P], high_1h[:, cols, :], low_1h[:, cols, :], start=False, stop=False)
                    T.matmul(bank[7][:, 0:P], high_1h[:, ECOLS - 4:ECOLS, :], low_1h[:, ECOLS - 4:ECOLS, :],
                             start=False, stop=True).then_inc(s_hist, 1)
                    pe.wait_ge(s_hist_ops, 1)
                if i == 6:
                    pe.wait_ge(s_hist_ops, 4)
                    pe.wait_ge(e_msged, i - 1)
                    T.matmul(bank[7][0:BUCKETS, 0:BUCKETS], same_high[:], hist_before[:], start=True, stop=False)
                    T.matmul(bank[7][0:BUCKETS, 0:BUCKETS], later_high[:], hist_total[:], start=False, stop=True)
                    T.matmul(bank[7][0:BUCKETS, BUCKETS:2 * BUCKETS], same_high[:], hist[:], start=True,
                             stop=True).then_inc(s_start_mm, 1)
                    pe.wait_ge(s_tiles_seen, 1)
                if i == 7:
                    pe.wait_ge(s_odd, 1)
                    pe.wait_ge(e_msged, i - 1)
                    T.matmul(bank[7][0:1, 0:1], ones32[:, 0:1], odd_sum[:], start=True, stop=True).then_inc(s_odd_mm, 1)
                    pe.wait_ge(s_general, 1)

            pe.wait_ge(s_const, 1)

            def hidden(i, m, t):
                if due(i):
                    pe.wait_ge(e_rlo, 4 * (i - 1) + t + 1)
                o = bank[2 + t][:]
                T.matmul(o, bias1[:, t, :], e_onehot[:, m % 4, :], start=True, stop=False)
                for k in range(2):
                    cols = slice((2 * t + k) * D, (2 * t + k + 1) * D)
                    last = product(o, w1_hi[:, cols], w1_lo[:, cols], e_h_hi[:, m % 2, k, :],
                                   e_h_lo[:, m % 2, k, :], False, k == 1)
                last.then_inc(e_l1, 1)

            def edge_step(i, m):
                g, s = i - 1, (m - 1) % 2
                if within(g, EG):
                    if due(g):
                        pe.wait_ge(e_msg_ted, g)
                    T.matmul(bank[6][:], bias2[:], e_onehot[:, (m - 1) % 4, :], start=True, stop=False)
                    for t in range(TYPES):
                        pe.wait_ge(e_rlo, 4 * g + t + 1)
                        last = product(bank[6][:], w2_hi[:, t * D:(t + 1) * D], w2_lo[:, t * D:(t + 1) * D],
                                       e_r_hi[:, s, t, :], e_r_lo[:, s, t, :], False, t == TYPES - 1)
                    last.then_inc(e_l2, 1)
                if within(i, EG):
                    pe.wait_ge(e_hlo, 2 * (i + 1))
                    pe.wait_ge(e_oh, i + 1)
                    for t in range(TYPES):
                        hidden(i, m, t)
                g, s = i + 1, (m + 1) % 2
                if within(g, EG):
                    pe.wait_ge(e_normed, g + 1)
                    if due(2 * g):
                        pe.wait_ge(e_hlo, 2 * g)
                    for k in range(2 * TILES):
                        last = T.transpose(bank[k // TILES][:, (k % TILES) * P:(k % TILES + 1) * P],
                                           e_h[:, s, k, :], ident[:])
                    last.then_inc(e_turned, 1)
                if isinstance(i, int):
                    count_tiles(i)
                g, s = i - 1, (m - 1) % 2
                if within(g, EG):
                    pe.wait_ge(e_msg_ted, g + 1)
                    if due(g):
                        pe.wait_ge(e_msged, g)
                    for k in range(TILES):
                        last = T.transpose(bank[7][:, k * D:(k + 1) * D], e_msg_t[:, s, k * P:(k + 1) * P], ident[:])
                    last.then_inc(e_back, 1)

            pipeline(pe, EG, -1, 1, edge_step)

            pe.wait_ge(e_msged, EG)
            with pe.If(pe.value_load(general[:], min_val=0, max_val=1) > 0):
                with pe.Fori(0, ECOLS) as c:
                    pe.wait_ge(g_spread, c + 1)
                    T.transpose(bank[6][:, 0:P], g_dst[:, 0:P], ident[:]).then_inc(g_across, 1)
                    pe.wait_ge(g_samed, c + 1)
                    pe.wait_ge(g_summed, c + 1)
                    T.matmul(bank[7][:, 0:D], g_same[:, 0:P], g_msg[:, 0:D], start=True, stop=True).then_inc(g_added, 1)

            def gate(b, row, s, sources):
                cols = slice(row * D, (row + 1) * D)
                for n, source in enumerate(sources):
                    w_hi, w_lo, v_hi, v_lo = {"h": (whh_hi, whh_lo, n_h_hi, n_h_lo),
                                              "a": (wih_hi, wih_lo, n_a_hi, n_a_lo)}[source]
                    last = product(bank[b][:], w_hi[:, cols], w_lo[:, cols], v_hi[:, s, :], v_lo[:, s, :],
                                   n == 0, n == len(sources) - 1)
                last.then_inc(n_gate, 1)

            def node_step(i, m):
                if within(i, NG):
                    pe.wait_ge(n_hlo, i + 1)
                    pe.wait_ge(n_alo, i + 1)
                    if due(i):
                        pe.wait_ge(n_red, i)
                    gate(3, 0, m % 2, "ha")
                    if due(i):
                        pe.wait_ge(n_ted, i)
                    gate(4, 2, m % 2, "h")
                g, s = i + 1, (m + 1) % 2
                if within(g, NG):
                    pe.wait_ge(n_normed, g + 1)
                    if due(g - 1):
                        pe.wait_ge(n_ded, g - 1)
                    for k in range(TILES):
                        last = T.transpose(bank[s][:, k * P:(k + 1) * P], n_h[:, s, k * D:(k + 1) * D], ident[:])
                    last.then_inc(n_turned, 1)
                    pe.wait_ge(n_seled, g + 1)
                    if due(g):
                        pe.wait_ge(n_alo, g)
                    for k in range(TILES):
                        last = T.matmul(bank[2][:, k * P:(k + 1) * P], n_win[:, (m + 1) % 4, k, 0:D],
                                        n_sel[:, s, k * P:(k + 1) * P], start=True, stop=True)
                    last.then_inc(n_summed, 1)
                if within(i, NG):
                    if due(i):
                        pe.wait_ge(n_ued, i)
                    gate(5, 2, m % 2, "a")
                    if due(i):
                        pe.wait_ge(n_zed, i)
                    gate(6, 1, m % 2, "ha")
                g, s = i - 1, (m - 1) % 2
                if within(g, NG):
                    pe.wait_ge(n_eed, g + 1)
                    if due(g):
                        pe.wait_ge(n_outed, g)
                    for k in range(TILES):
                        last = T.transpose(bank[7][:, k * P:(k + 1) * P], n_e[:, s, k * P:(k + 1) * P], ident[:])
                    last.then_inc(n_back, 1)

            pipeline(pe, NG, -1, 1, node_step)


def kernel(**inputs):
    import numpy as np
    import concourse.bacc as bacc
    from concourse.bass_utils import run_bass_kernel_spmd

    src, dst, types = (np.asarray(inputs[n]) for n in ("src", "dst", "edge_type_4"))
    edges = src.shape[0]
    eg = groups_of(edges)
    padded = np.zeros((3, eg * GROUP), np.int32)
    padded[0, :edges], padded[1, :edges], padded[2, :edges] = src, dst, types
    dst_marked = np.full(eg * GROUP, -1, np.int32)
    dst_marked[:edges] = dst
    arrays = {
        "x": np.ascontiguousarray(inputs["x"]),
        "edge_rows": np.ascontiguousarray(
            padded[0:2].reshape(2, eg, TILES, P).transpose(3, 1, 0, 2).reshape(P, eg, 2 * TILES)),
        "dst_cols": np.ascontiguousarray(dst_marked.reshape(eg * TILES, P).T),
        "dst_flat": np.append(dst_marked, np.int32(-1)),
        "types": padded[2:3],
        "W1": np.ascontiguousarray(inputs["L0_gnn_W1"]),
        "b1": np.ascontiguousarray(inputs["L0_gnn_b1"]),
        "W2": np.ascontiguousarray(inputs["L0_gnn_W2"]),
        "b2": np.ascontiguousarray(inputs["L0_gnn_b2"]),
        "WihT": np.ascontiguousarray(np.asarray(inputs["L0_gnn_W_ih"]).T),
        "WhhT": np.ascontiguousarray(np.asarray(inputs["L0_gnn_W_hh"]).T),
        "b_ih": np.ascontiguousarray(np.asarray(inputs["L0_gnn_b_ih"]).reshape(3, D).T),
        "b_hh": np.ascontiguousarray(np.asarray(inputs["L0_gnn_b_hh"]).reshape(3, D).T),
    }
    nc = bacc.Bacc("TRN2", target_bir_lowering=False, num_devices=1)
    args = [nc.dram_tensor(f"in_{name}", a.shape, mybir.dt.from_np(a.dtype), kind="ExternalInput").ap()
            for name, a in arrays.items()]
    out = nc.dram_tensor("out_0", arrays["x"].shape, F32, kind="ExternalOutput").ap()
    gnn_layer(nc, *args, out)
    r = run_bass_kernel_spmd(nc, [{f"in_{name}": a for name, a in arrays.items()}], core_ids=[0])
    return r.results[0]["out_0"]
```

```python
from contextlib import ExitStack

import concourse.bass as bass
from concourse import mybir

F32 = mybir.dt.float32
F32R = mybir.dt.float32r
I32 = mybir.dt.int32
ALU = mybir.AluOpType
ACT = mybir.ActivationFunctionType
AX_X = mybir.AxisListType.X

P = 128
D = 128
TYPES = 4
TILES = 4
GROUP = TILES * P
EPS = 1e-5
BIG = float(2 ** 100)
UNROLL = 4
HEAD = 8
SEL_DVE = 2
PITCH = 144
ROW = D + 1


def groups_of(rows):
    return -(-rows // GROUP)


def due(value):
    return not isinstance(value, int) or value > 0


def within(g, count):
    return not isinstance(g, int) or 0 <= g < count


def uses(g, slot, ring, inc):
    return (g - slot) * (inc // ring) + inc


def pipeline(eng, count, first, last, step):
    end = (count - UNROLL - 1) // UNROLL * UNROLL
    for i in range(first, HEAD):
        step(i, i % UNROLL)
    with eng.Fori(HEAD, end - UNROLL + 1, UNROLL) as i:
        for j in range(UNROLL):
            step(i + j, j)
    for i in range(end, count + last):
        step(i, i % UNROLL)


def gnn_layer(nc, x, edge_rows, dst_cols, dst_flat, types, W1, b1, W2, b2, WihT, WhhT, b_ih, b_hh, out):
    NODES = x.shape[0]
    NG = groups_of(NODES)
    EG = edge_rows.shape[1]
    ECOLS = EG * TILES
    EROWS = ECOLS * P

    TCOLS = -(-(NG * TILES + 1) // P)
    TABLE = TCOLS * P

    DENSE = EROWS
    messages = nc.dram_tensor("messages", (DENSE + NG * GROUP, PITCH), F32, kind="Internal").ap()
    node_sums = nc.dram_tensor("node_sums", (NG * GROUP + 1, D), F32, kind="Internal").ap()
    starts_dram = nc.dram_tensor("starts", (TABLE,), I32, kind="Internal").ap()

    ctx = ExitStack()
    with ctx:
        def sb(name, shape, dt=F32):
            return ctx.enter_context(nc.sbuf_tensor(name, shape, dt))

        def sem(name):
            return ctx.enter_context(nc.semaphore(name))

        iota_i = sb("iota_i", [P, P], I32)
        iota = sb("iota", [P, P])
        part_i = sb("part_i", [P, 1], I32)
        part = sb("part", [P, 1])
        ident = sb("ident", [P, P])
        tile_base_i = sb("tile_base_i", [P, TABLE], I32)
        tile_base = sb("tile_base", [P, TABLE])
        power = sb("power", [P, 2 * TILES])
        gathers_may_start = sb("gathers_may_start", [1, 1])
        ones128 = sb("ones128", [P, P])
        w1_hi = sb("w1_hi", [P, TYPES * 2 * D], F32R)
        w1_lo = sb("w1_lo", [P, TYPES * 2 * D], F32R)
        w2_hi = sb("w2_hi", [P, TYPES * D], F32R)
        w2_lo = sb("w2_lo", [P, TYPES * D], F32R)
        wih = sb("wih", [P, 3 * D])
        whh = sb("whh", [P, 3 * D])
        whh_hi = sb("whh_hi", [P, 3 * D], F32R)
        whh_lo = sb("whh_lo", [P, 3 * D], F32R)
        wih_hi = sb("wih_hi", [P, 3 * D], F32R)
        wih_lo = sb("wih_lo", [P, 3 * D], F32R)
        bih = sb("bih", [P, 3])
        bhh = sb("bhh", [P, 3])
        bsum = sb("bsum", [P, 3])
        bneg = sb("bneg", [P, 3])
        bias = sb("bias", [2 * TYPES, 2, D])
        bias_hi = sb("bias_hi", [2 * TYPES, 2, D], F32R)
        bias_lo = sb("bias_lo", [2 * TYPES, 2, D], F32R)
        bias_parts = sb("bias_parts", [2 * TYPES, 2, D])
        bias1 = sb("bias1", [2 * TYPES, TYPES, D], F32R)
        bias2 = sb("bias2", [2 * TYPES, D], F32R)
        r4_i = sb("r4_i", [2 * TYPES, 1], I32)
        r4 = sb("r4", [2 * TYPES, 1])
        upper = sb("upper", [2 * TYPES, 2])
        pick = sb("pick", [2 * TYPES, TYPES])
        minus_big = sb("minus_big", [2 * TYPES, TYPES])

        dst_i = sb("dst_i", [P, ECOLS], I32)
        dst_f = sb("dst_f", [P, ECOLS])
        last_f = sb("last_f", [P, 1])
        first_node = sb("first_node", [P, TCOLS], I32)
        rank_i = sb("rank_i", [P, TCOLS], I32)
        rank_f = sb("rank_f", [P, TCOLS])
        in_rank = sb("in_rank", [P, TCOLS])
        starts_i = sb("starts_i", [P, TCOLS], I32)
        starts = sb("starts_row", [1, TABLE], I32)
        odd = sb("odd", [P, 2])
        odd_sum = sb("odd_sum", [P, 1])
        general = sb("general", [1, 1], I32)
        g_row = sb("g_row", [P, 1], I32)

        rows_all = sb("rows_all", [P, EG, 2 * TILES], I32)
        rows_now = sb("rows_now", [P, 4, 2 * TILES], I32)
        e_x = sb("e_x", [P, 2, 2 * TILES, D])
        e_h = sb("e_h", [P, 2, 2 * TILES, D])
        e_h_hi = sb("e_h_hi", [P, 2, 2, GROUP], F32R)
        e_h_lo = sb("e_h_lo", [P, 2, 2, GROUP], F32R)
        e_r_hi = sb("e_r_hi", [P, 2, TYPES, GROUP], F32R)
        e_r_lo = sb("e_r_lo", [P, 2, TYPES, GROUP], F32R)
        e_type = sb("e_type", [2 * TYPES, 4, GROUP], I32)
        e_onehot = sb("e_onehot", [2 * TYPES, 4, GROUP], F32R)
        e_msg_t = sb("e_msg_t", [P, 2, GROUP])
        e_msg = sb("e_msg", [P, 4, TILES, ROW])
        raw = e_msg[:].rearrange("p a k d -> p (a k d)")
        w1 = raw[:, 0:TYPES * 2 * D]
        w2 = raw[:, TYPES * 2 * D:TYPES * 3 * D]

        bn = sb("bn", [P, 2 * TILES, 6])
        pair = sb("pair", [P, 2 * TILES, 2])
        diff = sb("diff", [P, 2 * TILES])
        minus_mean = sb("minus_mean", [P, 2, 2 * TILES])
        quarter = sb("quarter", [P, 2 * TILES])
        within_half = sb("within_half", [P, 2 * TILES])
        var = sb("var", [P, 2, 2 * TILES])
        std = sb("std", [P, 2, 2 * TILES])
        rstd = sb("rstd", [P, 2, 2 * TILES])
        shift = sb("shift", [P, 2, 2 * TILES])

        n_all = sb("n_all", [P, 20 * GROUP])
        taken = [0]

        def carve(ring, width):
            at = taken[0]
            taken[0] += ring * width
            return n_all[:, at:at + ring * width].rearrange("p (r w) -> p r w", r=ring)

        n_x = sb("n_x", [P, 4, GROUP])
        n_xh = e_h[:].rearrange("p a (b k) d -> p (a b) (k d)", b=2)
        n_h = carve(2, GROUP)
        n_sel = carve(2, GROUP)
        n_r = carve(2, GROUP)
        n_zc = carve(2, GROUP)
        n_t = carve(2, GROUP)
        n_n = carve(2, GROUP)
        n_d = carve(2, GROUP)
        n_e = carve(2, GROUP)
        n_out = carve(4, GROUP)
        n_win = sb("n_win", [P, 4, TILES, ROW])
        n_rel = sb("n_rel", [P, 2, TILES])
        n_h_hi = e_r_hi[:, 0, 0:2, :]
        n_h_lo = e_r_lo[:, 0, 0:2, :]
        n_a_hi = e_r_hi[:, 1, 0:2, :]
        n_a_lo = e_r_lo[:, 1, 0:2, :]
        taken_before = [0]

        def carve_before(columns, width):
            at = taken_before[0]
            taken_before[0] += columns * width
            return n_all[:, at:at + columns * width].rearrange("p (c w) -> p c w", c=columns)

        dst_two = carve_before(2, ECOLS).bitcast(I32)
        descends = carve_before(1, ECOLS)[:, 0, :]
        below = carve_before(1, TABLE)[:, 0, :]
        found = carve_before(TCOLS, ECOLS).bitcast(I32)
        smaller = carve_before(TCOLS, ECOLS)
        tile_count = carve_before(1, NG * TILES)[0:1, 0, :]
        g_all = n_out.rearrange("p r w -> p (r w)")
        g_blank = g_all[:, 0:TILES * PITCH].rearrange("p (k d) -> p k d", k=TILES)
        g_all = g_all[:, TILES * PITCH:]
        g_sum, g_dst, g_same, g_msg = (g_all[:, at:at + PITCH] for at in range(0, 4 * PITCH, PITCH))

        bank = [ctx.enter_context(nc.psum_tensor(f"bank{b}", [P, GROUP], F32)) for b in range(8)]

        s_weights = sem("s_weights")
        s_rows = sem("s_rows")
        s_dst = sem("s_dst")
        s_iota = sem("s_iota")
        s_const = sem("s_const")
        s_power = sem("s_power")
        s_split_hi = sem("s_split_hi")
        s_gate_weights = sem("s_gate_weights")
        s_prep = sem("s_prep")
        s_dst_two = sem("s_dst_two")
        s_count_ops = sem("s_count_ops")
        s_below = sem("s_below")
        s_rank_mm = sem("s_rank_mm")
        s_ranked = sem("s_ranked")
        s_found = sem("s_found")
        s_starts_i = sem("s_starts_i")
        s_starts_out = sem("s_starts_out")
        s_starts = sem("s_starts")
        s_odd = sem("s_odd")
        s_odd_mm = sem("s_odd_mm")
        s_general = sem("s_general")

        g_zeroed = sem("g_zeroed")
        g_blanked = sem("g_blanked")
        g_cleared = sem("g_cleared")
        g_zero_sums = sem("g_zero_sums")
        g_copied = sem("g_copied")
        g_loaded = sem("g_loaded")
        g_spread = sem("g_spread")
        g_across = sem("g_across")
        g_samed = sem("g_samed")
        g_added = sem("g_added")
        g_indexed = sem("g_indexed")
        g_steps = sem("g_steps")
        g_fetched = sem("g_fetched")
        g_summed = sem("g_summed")
        g_scattered = sem("g_scattered")

        e_staged = sem("e_staged")
        e_gated = sem("e_gated")
        e_gathered = [sem(f"e_gathered{s}") for s in range(2)]
        e_typed = [sem(f"e_typed{s}") for s in range(4)]
        e_stored = [sem(f"e_stored{s}") for s in range(4)]
        ln_ops = sem("ln_ops")
        e_var = sem("e_var")
        e_std = sem("e_std")
        e_recip = sem("e_recip")
        e_shift = sem("e_shift")
        e_normed = sem("e_normed")
        e_turned = sem("e_turned")
        e_hhi = sem("e_hhi")
        e_hlo = sem("e_hlo")
        e_oh = sem("e_oh")
        e_l1 = sem("e_l1")
        e_rhi = sem("e_rhi")
        e_rlo = sem("e_rlo")
        e_l2 = sem("e_l2")
        e_msg_ted = sem("e_msg_ted")
        e_back = sem("e_back")
        e_msged = sem("e_msged")
        e_dsted = sem("e_dsted")

        n_loaded = [sem(f"n_loaded{s}") for s in range(4)]
        n_windowed = [sem(f"n_windowed{s}") for s in range(4)]
        n_stored = [sem(f"n_stored{s}") for s in range(4)]
        n_var = sem("n_var")
        n_rstd = sem("n_rstd")
        n_shift = sem("n_shift")
        n_normed = sem("n_normed")
        n_reled = sem("n_reled")
        n_seled = sem("n_seled")
        n_seled_pool = sem("n_seled_pool")
        n_xhed = sem("n_xhed")
        n_turned = sem("n_turned")
        n_summed = sem("n_summed")
        n_hhi = sem("n_hhi")
        n_hlo = sem("n_hlo")
        n_ahi = sem("n_ahi")
        n_alo = sem("n_alo")
        n_gate = sem("n_gate")
        n_red = sem("n_red")
        n_zed = sem("n_zed")
        n_ted = sem("n_ted")
        n_ued = sem("n_ued")
        n_ned = sem("n_ned")
        n_ded = sem("n_ded")
        n_eed = sem("n_eed")
        n_back = sem("n_back")
        n_outed = sem("n_outed")

        N_WEIGHTS = 10
        N_SPLITS = 5
        LN_STEPS = 3
        block = ctx.enter_context(nc.Block())

        TAIL = NODES - (NG - 1) * GROUP
        parts = [(k, min(P, TAIL - k * P)) for k in range(TILES) if TAIL > k * P]

        def load_x(eng, g, s):
            if isinstance(g, int) and g == NG - 1:
                for k, rows in parts:
                    eng.dma_start(n_x[0:rows, s, k * D:(k + 1) * D],
                                 x[g * GROUP + k * P:g * GROUP + k * P + rows, :]).then_inc(n_loaded[s], 16)
            else:
                eng.dma_start(n_x[:, s, :].rearrange("p (k d) -> p k d", k=TILES),
                             x[bass.ds(g * GROUP, GROUP), :].rearrange("(k p) d -> p k d", p=P)
                             ).then_inc(n_loaded[s], 16)

        @block.sync
        def _(sp):
            sp.dma_start(rows_all[:], edge_rows).then_inc(s_rows, 16)
            sp.dma_start(dst_i[:], dst_cols).then_inc(s_dst, 16)
            for n in range(2):
                sp.dma_start(dst_two[:, n, :], dst_flat[n:n + EROWS].rearrange("(p c) -> p c", p=P)
                             ).then_inc(s_dst_two, 16)
            sp.dma_start(w1.rearrange("p (t k o) -> p t k o", t=TYPES, k=2),
                         W1.rearrange("t (k p) o -> p t k o", p=P)).then_inc(s_weights, 16)
            sp.dma_start(w2.rearrange("p (t o) -> p t o", t=TYPES),
                         W2.rearrange("t p o -> p t o")).then_inc(s_weights, 16)
            sp.dma_start(wih[:], WihT).then_inc(s_weights, 16)
            sp.dma_start(whh[:], WhhT).then_inc(s_weights, 16)
            sp.dma_start(bih[:], b_ih).then_inc(s_weights, 16)
            sp.dma_start(bhh[:], b_hh).then_inc(s_weights, 16)
            for copy in range(2):
                sp.dma_start(bias[copy * TYPES:(copy + 1) * TYPES, 0, :], b1).then_inc(s_weights, 16)
                sp.dma_start(bias[copy * TYPES:(copy + 1) * TYPES, 1, :], b2).then_inc(s_weights, 16)

            def edge_io(i, m):
                if isinstance(i, int) and i == EG - 4:
                    for first in range(4):
                        load_x(sp, first, first)
                g, s = i + 2, (m + 2) % 4
                if within(g, EG):
                    if due(g - 3):
                        sp.wait_ge(e_oh, g - 3)
                    sp.dma_start(e_type[:, s, :], types[:, bass.ds(g * GROUP, GROUP)]
                                 .to_broadcast([2 * TYPES, GROUP])).then_inc(e_typed[s], 16)
                g, s = i - 3, (m - 3) % 4
                if within(g, EG):
                    sp.wait_ge(e_msged, g + 1)
                    sp.wait_ge(e_dsted, g + 1)
                    sp.dma_start(messages[bass.ds(g * GROUP, GROUP), 0:ROW].rearrange("(k p) d -> p k d", p=P),
                                 e_msg[:, s]).then_inc(e_stored[s], 16)
                if isinstance(i, int) and i == 7:
                    sp.wait_ge(s_starts_i, 1)
                    sp.dma_start(starts_dram.rearrange("(p c) -> p c", p=P), starts_i[:]
                                 ).then_inc(s_starts_out, 16)
                    sp.wait_ge(s_starts_out, 16)
                    sp.dma_start(starts[:], starts_dram.rearrange("(a n) -> a n", a=1)).then_inc(s_starts, 16)

            pipeline(sp, EG, -2, 3, edge_io)
            for s in range(4):
                sp.wait_ge(e_stored[s], uses((EG - 1 - s) // 4 * 4 + s, s, 4, 16))
            sp.wait_ge(s_starts, 16)

            sp.wait_ge(s_general, 1)
            with sp.If(sp.value_load(general[:], min_val=0, max_val=1) > 0):
                with sp.Fori(0, NG) as g:
                    sp.wait_ge(g_blanked, g + 1)
                    sp.dma_start(messages[bass.ds(g * GROUP + DENSE, GROUP), 0:ROW].rearrange("(k p) d -> p k d", p=P),
                                 g_blank[:, :, 0:ROW]).then_inc(g_cleared, 16)
                    sp.dma_start(node_sums[bass.ds(g * GROUP, GROUP), :].rearrange("(k p) d -> p k d", p=P),
                                 g_blank[:, :, 0:D]).then_inc(g_zero_sums, 16)
                sp.dma_start(node_sums[NG * GROUP:NG * GROUP + 1, :], g_blank[0:1, 0, 0:D]).then_inc(g_zero_sums, 16)
                with sp.Fori(0, ECOLS) as c:
                    sp.wait_ge(g_summed, c + 1)
                    sp.dma_start(g_msg[:, 0:ROW], messages[bass.ds(c * P, P), 0:ROW]).then_inc(g_loaded, 16)
                sp.wait_ge(g_steps, 3 * ECOLS + 1)
                with sp.Fori(0, NG) as g:
                    sp.dma_start(messages[bass.ds(g * GROUP + DENSE, GROUP), 0:D],
                                 node_sums[bass.ds(g * GROUP, GROUP), :]).then_inc(g_copied, 16)
                sp.wait_ge(g_cleared, 16 * NG)
                sp.wait_ge(g_copied, 16 * NG)

            def node_io(i, m):
                g, s = i + 4, m % 4
                if within(g, NG):
                    if due(g - 3):
                        sp.wait_ge(n_summed, g - 3)
                    for k in range(TILES):
                        start = sp.value_load(starts[0:1, bass.ds(g * TILES + k, 1)],
                                              min_val=0, max_val=DENSE + NG * GROUP - P)
                        sp.dma_start(n_win[:, s, k, :], messages[bass.ds(start, P), 0:ROW]
                                     ).then_inc(n_windowed[s], 16)
                g, s = i - 2, (m - 2) % 4
                if within(g, NG):
                    sp.wait_ge(n_outed, g + 1)
                    if isinstance(g, int) and g == NG - 1:
                        for k, rows in parts:
                            sp.dma_start(out[g * GROUP + k * P:g * GROUP + k * P + rows, :],
                                         n_out[0:rows, s, k * D:(k + 1) * D]).then_inc(n_stored[s], 16)
                    else:
                        sp.dma_start(out[bass.ds(g * GROUP, GROUP), :].rearrange("(k p) d -> p k d", p=P),
                                     n_out[:, s, :].rearrange("p (k d) -> p k d", k=TILES)
                                     ).then_inc(n_stored[s], 16)

            pipeline(sp, NG, -4, 2, node_io)
            for s in range(4):
                last = (NG - 1 - s) // 4 * 4 + s
                extra = 16 * (len(parts) - 1) if last == NG - 1 else 0
                sp.wait_ge(n_stored[s], uses(last, s, 4, 16) + extra)

        @block.gpsimd
        def _(pool):
            nc.gpsimd.iota(iota_i[:], pattern=[[1, P]], base=0, channel_multiplier=0)
            nc.gpsimd.iota(tile_base_i[:], pattern=[[P, TABLE]], base=0, channel_multiplier=0)
            nc.gpsimd.iota(first_node[:], pattern=[[P, TCOLS]], base=0, channel_multiplier=P * TCOLS)
            nc.gpsimd.iota(part_i[:, 0:1], pattern=[[0, 1]], base=0, channel_multiplier=1).then_inc(s_iota, 1)

            nc.gpsimd.memset(power[:], -0.5).then_inc(s_power, 1)
            pool.wait_ge(s_power, 1)

            def stage(g, s):
                nc.gpsimd.tensor_copy(rows_now[:, s, :], rows_all[:, bass.ds(g, 1), :]
                                      .rearrange("p a k -> p (a k)")).then_inc(e_staged, 1)

            pool.wait_ge(s_rows, 16)
            stage(0, 0)

            def gather(g, m):
                if within(g + 1, EG):
                    stage(g + 1, (m + 1) % 4)
                pool.wait_ge(e_staged, g + 1)
                if due(g):
                    pool.wait_ge(e_gated, g)
                if due(g - 1):
                    pool.wait_ge(e_normed, g - 1)
                nc.gpsimd.tensor_tensor(gathers_may_start[:], power[0:1, 0:1], power[0:1, 0:1],
                                        ALU.add).then_inc(e_gated, 1)
                for k in range(2 * TILES):
                    nc.gpsimd.indirect_dma_start(
                        e_x[:, m % 2, k, :], None, x,
                        bass.IndirectOffsetOnAxis(ap=rows_now[:, m % 4, k:k + 1], axis=0)
                    ).then_inc(e_gathered[m % 2], 16)
                if isinstance(g, int) and g == 4:
                    pool.wait_ge(s_ranked, 2)
                    for c in range(TCOLS):
                        nc.gpsimd.indirect_dma_start(
                            found[:, c, :], None, dst_flat[0:EROWS].rearrange("(p c) -> p c", p=P),
                            bass.IndirectOffsetOnAxis(ap=rank_i[:, c:c + 1], axis=0)).then_inc(s_found, 16)

            pipeline(pool, EG, 0, 0, gather)

            pool.wait_ge(s_general, 1)
            with pool.If(pool.value_load(general[:], min_val=0, max_val=1) > 0):

                def step(value=None):
                    if value is not None:
                        pool.wait_ge(g_steps, value)
                    nc.gpsimd.tensor_tensor(gathers_may_start[:], power[0:1, 0:1], power[0:1, 0:1],
                                            ALU.add).then_inc(g_steps, 1)

                pool.wait_ge(g_zero_sums, 16 * (NG + 1))
                pool.wait_ge(e_gated, EG)
                step()
                with pool.Fori(0, ECOLS) as c:
                    pool.wait_ge(g_indexed, c + 1)
                    step(3 * c + 1)
                    nc.gpsimd.indirect_dma_start(g_sum[:, 0:D], None, node_sums,
                                                 bass.IndirectOffsetOnAxis(ap=g_row[:], axis=0)).then_inc(g_fetched, 16)
                    pool.wait_ge(g_summed, c + 2)
                    step(3 * c + 2)
                    nc.gpsimd.indirect_dma_start(node_sums, bass.IndirectOffsetOnAxis(ap=g_row[:], axis=0),
                                                 g_sum[:, 0:D], None).then_inc(g_scattered, 16)
                    pool.wait_ge(g_scattered, 16 * c + 16)
                    step(3 * c + 3)

            def reciprocals(g, s):
                pool.wait_ge(n_var, g + 1)
                if due(g - 1):
                    pool.wait_ge(n_normed, g - 1)
                nc.gpsimd.tensor_tensor(rstd[:, s % 2, 0:TILES], var[:, s % 2, 0:TILES], power[:, 0:TILES],
                                        ALU.pow).then_inc(n_rstd, 1)
                pool.wait_ge(n_rstd, g + 1)
                nc.gpsimd.tensor_tensor(shift[:, s % 2, 0:TILES], minus_mean[:, s % 2, 0:TILES],
                                        rstd[:, s % 2, 0:TILES], ALU.mult).then_inc(n_shift, 1)

            def select_tiles(eng, s):
                for k in range(SEL_DVE, TILES):
                    last = eng.tensor_scalar(n_sel[:, s, k * P:(k + 1) * P], iota[:], n_rel[:, s, k:k + 1], None,
                                             ALU.is_equal)
                return last

            def node_side(i, m):
                g, s = i - 1, (m - 1) % 2
                if within(g, NG):
                    pool.wait_ge(n_ded, g + 1)
                    pool.wait_ge(n_zed, g + 1)
                    if due(g - 1):
                        pool.wait_ge(n_back, g - 1)
                    nc.gpsimd.tensor_tensor(n_e[:, s, :], n_d[:, s, :], n_zc[:, s, :], ALU.mult).then_inc(n_eed, 1)
                g, s = i + 2, (m + 2) % 4
                if within(g, NG) and not (isinstance(g, int) and g < 2):
                    reciprocals(g, s)
                g, s = i + 3, (m + 3) % 4
                if within(g, NG):
                    pool.wait_ge(n_windowed[s], uses(g, s, 4, 64))
                    if due(g - 1):
                        pool.wait_ge(n_seled, g - 1)
                        pool.wait_ge(n_seled_pool, g - 1)
                    nc.gpsimd.tensor_tensor(
                        n_rel[:, s % 2, :], n_win[:, s, :, D:ROW].rearrange("p k a -> p (k a)"),
                        tile_base[:, bass.ds(g * TILES, TILES)], ALU.subtract).then_inc(n_reled, 1)
                if isinstance(i, int) and i == -2:
                    pool.wait_ge(n_reled, 1)
                    nc.gpsimd.tensor_tensor(gathers_may_start[:], power[0:1, 0:1], power[0:1, 0:1],
                                            ALU.add)
                    select_tiles(nc.gpsimd, 0).then_inc(n_seled_pool, 1)
                g, s = i + 1, (m + 1) % 4
                if within(g, NG):
                    pool.wait_ge(n_normed, g + 1)
                    if due(g - 3):
                        pool.wait_ge(n_outed, g - 3)
                    if within(g + 1, NG):
                        pool.wait_ge(n_reled, g + 2)
                    if due(g):
                        pool.wait_ge(n_summed, g)
                    nc.gpsimd.tensor_tensor(n_xh[:, s, :], n_h[:, s % 2, :], n_x[:, s, :], ALU.add).then_inc(n_xhed, 1)
                    if within(g + 1, NG):
                        select_tiles(nc.gpsimd, (m + 2) % 2).then_inc(n_seled_pool, 1)

            reciprocals(0, 0)
            reciprocals(1, 1)
            pipeline(pool, NG, -3, 1, node_side)

        @block.vector
        def _(dve):
            chain = [0]

            def link(ins):
                chain[0] += 1
                ins.then_inc(s_prep, 1)
                dve.wait_ge(s_prep, chain[0])

            V = nc.vector
            dve.wait_ge(s_iota, 1)
            V.tensor_copy(iota[:], iota_i[:])
            V.tensor_copy(tile_base[:], tile_base_i[:])
            V.memset(ones128[:], 1.0)
            link(V.tensor_scalar(r4_i[:], part_i[0:2 * TYPES, 0:1], TYPES - 1, None, ALU.bitwise_and))
            V.tensor_copy(r4[:], r4_i[:])
            link(V.tensor_copy(part[:], part_i[:]))
            V.tensor_scalar(pick[:], iota[0:2 * TYPES, 0:TYPES], r4[:], None, ALU.is_equal)
            V.tensor_scalar(upper[:, 0:1], part[0:2 * TYPES, 0:1], float(TYPES), None, ALU.is_lt)
            V.tensor_scalar(upper[:, 1:2], part[0:2 * TYPES, 0:1], float(TYPES), None, ALU.is_ge)
            link(V.tensor_scalar(ident[:], iota[:], part[:, 0:1], None, ALU.is_equal))
            link(V.tensor_scalar(minus_big[:], pick[:], BIG, -BIG, ALU.mult, ALU.add))
            link(V.tensor_scalar(minus_big[:], minus_big[:], upper[:, 0:1], None, ALU.mult))
            dve.wait_ge(s_weights, 16 * N_WEIGHTS)
            dve.wait_ge(s_split_hi, 3)
            V.tensor_tensor(w1_lo[:], w1, w1_hi[:].bitcast(F32), ALU.subtract)
            V.tensor_tensor(w2_lo[:], w2, w2_hi[:].bitcast(F32), ALU.subtract)
            link(V.tensor_tensor(bias_lo[:], bias[:], bias_hi[:].bitcast(F32), ALU.subtract))
            link(V.tensor_scalar(bias_parts[:], bias_hi[:].bitcast(F32), upper[:, 0:1], None, ALU.mult))
            link(V.scalar_tensor_tensor(out=bias_parts[:], in0=bias_lo[:].bitcast(F32), scalar=upper[:, 1:2],
                                        in1=bias_parts[:], op0=ALU.mult, op1=ALU.add))
            V.tensor_copy(bias2[:], bias_parts[:, 1, :])
            for t in range(TYPES):
                V.tensor_scalar(bias1[:, t, :], bias_parts[:, 0, :], pick[:, t:t + 1], minus_big[:, t:t + 1],
                                ALU.mult, ALU.add)
            link(V.tensor_tensor(bsum[:], bih[:], bhh[:], ALU.add))
            V.tensor_scalar(bneg[:], bsum[:], -1.0, None, ALU.mult).then_inc(s_const, 1)

            V.memset(odd[:], 0.0)
            dve.wait_ge(s_dst, 16)
            V.tensor_copy(dst_f[:], dst_i[:])
            done = [0]

            def count_link(ins):
                done[0] += 1
                ins.then_inc(s_count_ops, 1)
                dve.wait_ge(s_count_ops, done[0])

            def find_starts(i):
                if i == 0:
                    dve.wait_ge(s_dst_two, 32)
                    count_link(V.tensor_copy(last_f[:], dst_two[:, 0, ECOLS - 1:ECOLS]))
                    V.tensor_scalar(below, tile_base[:], last_f[:], None, ALU.is_gt).then_inc(s_below, 1)
                    count_link(V.tensor_tensor(descends, dst_two[:, 0, :], dst_two[:, 1, :], ALU.is_gt))
                    V.tensor_reduce(odd[:, 0:1], descends, AX_X, ALU.add)
                if i == 1:
                    dve.wait_ge(s_rank_mm, 1)
                    V.tensor_copy(rank_f[:], bank[7][:, 0:TCOLS]).then_inc(s_ranked, 1)
                    V.tensor_copy(rank_i[:], bank[7][:, 0:TCOLS]).then_inc(s_ranked, 1)
                if i == 2:
                    dve.wait_ge(s_split_hi, N_SPLITS)
                    V.tensor_tensor(whh_lo[:], whh[:], whh_hi[:].bitcast(F32), ALU.subtract)
                if i == 3:
                    V.tensor_tensor(wih_lo[:], wih[:], wih_hi[:].bitcast(F32), ALU.subtract).then_inc(s_gate_weights, 1)
                if i == 5:
                    dve.wait_ge(s_found, 16 * TCOLS)
                    count_link(V.tensor_tensor(smaller, found,
                                               first_node[:].unsqueeze(2).to_broadcast([P, TCOLS, ECOLS]), ALU.is_lt))
                if i == 6:
                    count_link(V.tensor_reduce(in_rank[:], smaller, AX_X, ALU.add))
                    V.scalar_tensor_tensor(out=starts_i[:], in0=rank_f[:], scalar=float(ECOLS), in1=in_rank[:],
                                           op0=ALU.mult, op1=ALU.add).then_inc(s_starts_i, 1)
                if i == EG - 5:
                    dve.wait_ge(s_starts, 16)
                    count_link(V.tensor_tensor(tile_count, starts[0:1, 1:NG * TILES + 1], starts[0:1, 0:NG * TILES],
                                               ALU.subtract))
                    count_link(V.tensor_scalar(tile_count, tile_count, float(P), None, ALU.is_gt))
                    count_link(V.tensor_reduce(odd[0:1, 1:2], tile_count, AX_X, ALU.add))
                    V.tensor_reduce(odd_sum[:], odd[:], AX_X, ALU.add).then_inc(s_odd, 1)
                if i == EG - 4:
                    dve.wait_ge(s_odd_mm, 1)
                    V.tensor_scalar(general[:], bank[7][0:1, 0:1], 0.5, None, ALU.is_gt).then_inc(s_general, 1)

            def ln_rows(count, tile):
                for k in range(count):
                    last = V.bn_stats(bn[:, k, :], tile(k))
                last.then_inc(ln_ops, 1)

            def ln_stats(count, slot, base, finish):
                done = [base + 1]
                dve.wait_ge(ln_ops, done[0])

                def ln_link(ins):
                    done[0] = done[0] + 1
                    ins.then_inc(ln_ops, 1)
                    dve.wait_ge(ln_ops, done[0])

                halves = bn[:, 0:count, :].rearrange("p k (h c) -> p k h c", h=2)
                V.tensor_tensor(pair[:, 0:count, :], halves[:, :, 0, 1:3], halves[:, :, 1, 1:3], ALU.add)
                ln_link(V.tensor_tensor(diff[:, 0:count], bn[:, 0:count, 1], bn[:, 0:count, 4], ALU.subtract))
                V.tensor_scalar(minus_mean[:, slot, 0:count], pair[:, 0:count, 0], -0.5, None, ALU.mult)
                V.tensor_scalar(within_half[:, 0:count], pair[:, 0:count, 1], 1.0 / D, EPS, ALU.mult, ALU.add)
                ln_link(V.scalar_tensor_tensor(out=quarter[:, 0:count], in0=diff[:, 0:count], scalar=0.25,
                                               in1=diff[:, 0:count], op0=ALU.mult, op1=ALU.mult))
                V.tensor_tensor(var[:, slot, 0:count], within_half[:, 0:count], quarter[:, 0:count],
                                ALU.add).then_inc(finish, 1)

            def low_hidden(i, m, t):
                dve.wait_ge(e_rhi, 4 * i + t + 1)
                if t == 0 and due(i - 1):
                    dve.wait_ge(e_l2, i - 1)
                V.scalar_tensor_tensor(out=e_r_lo[:, m % 2, t, :], in0=bank[2 + t][:], scalar=0.0,
                                       in1=e_r_hi[:, m % 2, t, :].bitcast(F32), op0=ALU.max,
                                       op1=ALU.subtract).then_inc(e_rlo, 1)

            def edge_stats(g, s):
                dve.wait_ge(e_gathered[s], uses(g, s, 2, 16 * 2 * TILES))
                ln_rows(2 * TILES, lambda k: e_x[:, s, k, :])
                ln_stats(2 * TILES, s, g * LN_STEPS, e_var)

            def edge_reciprocals(g, s):
                dve.wait_ge(e_std, g + 1)
                if due(g - 1):
                    dve.wait_ge(e_normed, g - 1)
                V.reciprocal(rstd[:, s, :], std[:, s, :]).then_inc(e_recip, 1)
                dve.wait_ge(e_recip, g + 1)
                V.tensor_tensor(shift[:, s, :], minus_mean[:, s, :], rstd[:, s, :], ALU.mult).then_inc(e_shift, 1)

            def edge_step(i, m):
                g, s = i - 1, (m - 1) % 4
                if within(g, EG):
                    if due(g - 3):
                        dve.wait_ge(e_stored[s], uses(g - 4, s, 4, 16))
                    V.tensor_copy(e_msg[:, s, :, D:ROW].rearrange("p k a -> p (k a)"),
                                  dst_f[:, bass.ds(g * TILES, TILES)]).then_inc(e_dsted, 1)
                g, s = i + 1, (m + 1) % 4
                if within(g, EG):
                    dve.wait_ge(e_typed[s], uses(g, s, 4, 16))
                    if due(g - 3):
                        dve.wait_ge(e_l2, g - 3)
                    V.tensor_scalar(e_onehot[:, s, :], e_type[:, s, :], r4[:], None, ALU.is_equal).then_inc(e_oh, 1)
                g, s = i + 2, (m + 2) % 2
                first = isinstance(i, int) and i == -1
                if within(g, EG) and not first:
                    edge_stats(g, s)
                if within(i, EG):
                    for t in range(3):
                        low_hidden(i, m, t)
                if within(g, EG) and not first:
                    edge_reciprocals(g, s)
                if within(i, EG):
                    low_hidden(i, m, 3)
                g, s = i + 1, (m + 1) % 2
                if within(g, EG):
                    for half_ in range(2):
                        dve.wait_ge(e_hhi, 2 * g + half_ + 1)
                        if half_ == 0 and due(g - 1):
                            dve.wait_ge(e_l1, 4 * (g - 1))
                        V.tensor_tensor(e_h_lo[:, s, half_, :], bank[half_][:],
                                        e_h_hi[:, s, half_, :].bitcast(F32), ALU.subtract).then_inc(e_hlo, 1)
                if first:
                    edge_stats(1, 1)
                    edge_reciprocals(1, 1)
                if isinstance(i, int):
                    find_starts(i)

            pipeline(dve, EG, -2, 1, edge_step)

            dve.wait_ge(s_general, 1)
            with dve.If(dve.value_load(general[:], min_val=0, max_val=1) > 0):
                dve.wait_ge(s_starts, 16)
                V.tensor_scalar(starts[:], tile_base_i[0:1, :], DENSE, None,
                                ALU.add).then_inc(g_summed, 1)
                V.memset(g_blank, 0.0).then_inc(g_zeroed, 1)
                dve.wait_ge(g_zeroed, 1)
                V.tensor_scalar(g_blank[:, :, D], tile_base[:, 0:TILES], part[:, 0:1], None,
                                ALU.add).then_inc(g_blanked, 1)
                with dve.Fori(1, NG) as g:
                    dve.wait_ge(g_cleared, 16 * g)
                    V.tensor_scalar(g_blank[:, :, D], tile_base[:, bass.ds(g * TILES, TILES)], part[:, 0:1], None,
                                    ALU.add).then_inc(g_blanked, 1)
                with dve.Fori(0, ECOLS) as c:
                    dve.wait_ge(g_loaded, 16 * c + 16)
                    dve.wait_ge(g_steps, 3 * c + 1)
                    V.tensor_copy(g_row[:], g_msg[:, D:ROW]).then_inc(g_indexed, 1)
                    V.tensor_scalar(g_dst[:, 0:P], ones128[:], g_msg[:, D:ROW], None, ALU.mult).then_inc(g_spread, 1)
                    dve.wait_ge(g_across, c + 1)
                    V.tensor_scalar(g_same[:, 0:P], bank[6][:, 0:P], g_msg[:, D:ROW], None,
                                    ALU.is_equal).then_inc(g_samed, 1)
                    dve.wait_ge(g_added, c + 1)
                    dve.wait_ge(g_fetched, 16 * c + 16)
                    V.tensor_tensor(g_sum[:, 0:D], g_sum[:, 0:D], bank[7][:, 0:D], ALU.add).then_inc(g_summed, 1)

            def node_rows(g, s):
                tail = isinstance(g, int) and g == NG - 1
                dve.wait_ge(n_loaded[s], uses(g, s, 4, 16) + (16 * (-(-(NODES - g * GROUP) // P) - 1) if tail else 0))
                ln_rows(TILES, lambda k: n_x[:, s, k * D:(k + 1) * D])

            def node_stats(g, s):
                if due(g - 1):
                    dve.wait_ge(n_shift, g - 1)
                ln_stats(TILES, s, EG * LN_STEPS + g * LN_STEPS, n_var)

            def node_step(i, m):
                g, s = i, m % 2
                if within(g, NG):
                    dve.wait_ge(n_red, g + 1)
                    dve.wait_ge(n_gate, 4 * g + 2)
                    if due(g - 1):
                        dve.wait_ge(n_ned, g - 1)
                    V.scalar_tensor_tensor(out=n_t[:, s, :], in0=bank[4][:], scalar=bhh[:, 2:3], in1=n_r[:, s, :],
                                           op0=ALU.add, op1=ALU.mult).then_inc(n_ted, 1)
                g, s = i + 2, (m + 2) % 2
                if within(g, NG):
                    dve.wait_ge(n_reled, g + 1)
                    if due(g - 1):
                        dve.wait_ge(n_summed, g - 1)
                    V.tensor_tensor(n_sel[:, s, 0:SEL_DVE * P].rearrange("p (k n) -> p k n", k=SEL_DVE),
                                    iota[:].unsqueeze(1).to_broadcast([P, SEL_DVE, P]),
                                    n_rel[:, s, 0:SEL_DVE].unsqueeze(2).to_broadcast([P, SEL_DVE, P]),
                                    ALU.is_equal).then_inc(n_seled, 1)
                g, s = i + 1, (m + 1) % 2
                if within(g, NG):
                    dve.wait_ge(n_hhi, g + 1)
                    if due(g - 1):
                        dve.wait_ge(n_gate, 4 * (g - 1))
                    V.tensor_tensor(n_h_lo[:, s, :], bank[s][:], n_h_hi[:, s, :].bitcast(F32),
                                    ALU.subtract).then_inc(n_hlo, 1)
                    dve.wait_ge(n_ahi, g + 1)
                    V.tensor_tensor(n_a_lo[:, s, :], bank[2][:], n_a_hi[:, s, :].bitcast(F32),
                                    ALU.subtract).then_inc(n_alo, 1)
                g, s = i, m % 2
                if within(g, NG):
                    dve.wait_ge(n_gate, 4 * g + 3)
                    dve.wait_ge(n_ted, g + 1)
                    V.tensor_tensor(n_t[:, s, :], bank[5][:], n_t[:, s, :], ALU.add).then_inc(n_ued, 1)
                g, s = i + 3, (m + 3) % 4
                if within(g, NG) and not (isinstance(g, int) and g < 2):
                    node_rows(g, s)
                g, s = i, m % 2
                if within(g, NG):
                    dve.wait_ge(n_ned, g + 1)
                    if due(g - 1):
                        dve.wait_ge(n_eed, g - 1)
                    V.tensor_tensor(n_d[:, s, :], bank[s][:], n_n[:, s, :], ALU.subtract).then_inc(n_ded, 1)
                g, s = i + 3, (m + 3) % 2
                if within(g, NG) and not (isinstance(g, int) and g < 2):
                    node_stats(g, s)
                g, s = i - 1, (m - 1) % 4
                if within(g, NG):
                    dve.wait_ge(n_back, g + 1)
                    if due(g - 3):
                        dve.wait_ge(n_stored[s], uses(g - 4, s, 4, 16))
                    V.tensor_tensor(n_out[:, s, :], n_xh[:, s, :], bank[7][:], ALU.subtract).then_inc(n_outed, 1)

            for g in range(2):
                node_rows(g, g)
                node_stats(g, g)
            pipeline(dve, NG, -3, 1, node_step)

        @block.scalar
        def _(act):
            A = nc.scalar
            act.wait_ge(s_weights, 16 * N_WEIGHTS)
            for full, high in ((w1, w1_hi), (w2, w2_hi), (bias[:], bias_hi)):
                A.activation(high[:], full, ACT.Copy).then_inc(s_split_hi, 1)

            def high_hidden(i, m, t):
                act.wait_ge(e_l1, 4 * i + t + 1)
                A.activation(e_r_hi[:, m % 2, t, :], bank[2 + t][:], ACT.Relu).then_inc(e_rhi, 1)

            def deviations(g, s):
                act.wait_ge(e_var, g + 1)
                A.activation(std[:, s, :], var[:, s, :], ACT.Sqrt).then_inc(e_std, 1)

            def normalise_edges(g, s, tiles):
                if not within(g, EG):
                    return
                if 0 in tiles:
                    act.wait_ge(e_shift, g + 1)
                    if due(g - 1):
                        act.wait_ge(e_turned, g - 1)
                for k in tiles:
                    last = A.activation(e_h[:, s, k, :], e_x[:, s, k, :], ACT.Relu, scale=rstd[:, s, k:k + 1],
                                        bias=shift[:, s, k:k + 1])
                if 2 * TILES - 1 in tiles:
                    last.then_inc(e_normed, 1)

            def edge_step(i, m):
                g, s = i - 2, (m - 2) % 4
                if within(g, EG):
                    act.wait_ge(e_back, g + 1)
                    if due(g - 3):
                        act.wait_ge(e_stored[s], uses(g - 4, s, 4, 16))
                    A.activation(e_msg[:, s, :, 0:D], bank[7][:].rearrange("p (k d) -> p k d", k=TILES),
                                 ACT.Copy).then_inc(e_msged, 1)
                normalise_edges(i + 1, (m + 1) % 2, (0, 1, 2, 3, 4))
                g, s = i - 1, (m - 1) % 2
                if within(g, EG):
                    act.wait_ge(e_l2, g + 1)
                    A.activation(e_msg_t[:, s, :], bank[6][:], ACT.Copy).then_inc(e_msg_ted, 1)
                normalise_edges(i + 1, (m + 1) % 2, (5, 6, 7))
                if within(i, EG):
                    high_hidden(i, m, 0)
                    high_hidden(i, m, 1)
                first = isinstance(i, int) and i == -1
                if within(i + 2, EG) and not first:
                    deviations(i + 2, m % 2)
                if within(i, EG):
                    high_hidden(i, m, 2)
                    high_hidden(i, m, 3)
                g, s = i + 1, (m + 1) % 2
                if within(g, EG):
                    act.wait_ge(e_turned, g + 1)
                    for half_ in range(2):
                        A.activation(e_h_hi[:, s, half_, :], bank[half_][:], ACT.Copy).then_inc(e_hhi, 1)
                if first:
                    deviations(1, 1)
                if isinstance(i, int) and i == 1:
                    for full, high in ((whh[:], whh_hi), (wih[:], wih_hi)):
                        A.activation(high[:], full, ACT.Copy).then_inc(s_split_hi, 1)

            pipeline(act, EG, -2, 2, edge_step)

            def normalise(i, m, tiles):
                g, s = i, m % 4
                if not within(g, NG):
                    return
                if 0 in tiles:
                    act.wait_ge(n_shift, g + 1)
                    if due(g - 1):
                        act.wait_ge(n_turned, g - 1)
                        act.wait_ge(n_xhed, g - 1)
                for k in tiles:
                    cols = slice(k * D, (k + 1) * D)
                    last = A.activation(n_h[:, s % 2, cols], n_x[:, s, cols], ACT.Relu,
                                        scale=rstd[:, s % 2, k:k + 1], bias=shift[:, s % 2, k:k + 1])
                if TILES - 1 in tiles:
                    last.then_inc(n_normed, 1)

            def node_step(i, m):
                g, s = i + 4, m % 4
                if within(g, NG) and due(g - 3):
                    act.wait_ge(n_xhed, g - 3)
                    load_x(act, g, s)
                normalise(i + 1, m + 1, (3,))
                g, s = i, m % 2
                if within(g, NG):
                    act.wait_ge(n_gate, 4 * g + 1)
                    if due(g - 1):
                        act.wait_ge(n_ted, g - 1)
                    A.activation(n_r[:, s, :], bank[3][:], ACT.Sigmoid, bias=bsum[:, 0:1]).then_inc(n_red, 1)
                g, s = i + 1, (m + 1) % 2
                if within(g, NG):
                    act.wait_ge(n_turned, g + 1)
                    if due(g - 1):
                        act.wait_ge(n_gate, 4 * (g - 1))
                    A.activation(n_h_hi[:, s, :], bank[s][:], ACT.Copy).then_inc(n_hhi, 1)
                    act.wait_ge(n_summed, g + 1)
                    A.activation(n_a_hi[:, s, :], bank[2][:], ACT.Copy).then_inc(n_ahi, 1)
                normalise(i + 2, m + 2, (0, 1, 2))
                g, s = i, m % 2
                if within(g, NG):
                    act.wait_ge(n_ued, g + 1)
                    if due(g - 1):
                        act.wait_ge(n_ded, g - 1)
                    A.activation(n_n[:, s, :], n_t[:, s, :], ACT.Tanh, bias=bih[:, 2:3]).then_inc(n_ned, 1)
                    act.wait_ge(n_gate, 4 * g + 4)
                    if due(g - 1):
                        act.wait_ge(n_eed, g - 1)
                    A.activation(n_zc[:, s, :], bank[6][:], ACT.Sigmoid, bias=bneg[:, 1:2],
                                 scale=-1.0).then_inc(n_zed, 1)

            pipeline(act, NG, -2, 1, node_step)

        @block.tensor
        def _(pe):
            T = nc.tensor

            def product(o, w_hi, w_lo, v_hi, v_lo, start, stop, **kw):
                T.matmul(o, w_hi, v_hi, start=start, stop=False, **kw)
                T.matmul(o, w_hi, v_lo, start=False, stop=False, **kw)
                return T.matmul(o, w_lo, v_hi, start=False, stop=stop, **kw)

            def find_starts(i):
                if i == 1:
                    pe.wait_ge(s_below, 1)
                    for c in range(TCOLS):
                        last = T.matmul(bank[7][:, c:c + 1], below[0:P - 1, c::TCOLS], ones128[0:P - 1, 0:1],
                                        start=True, stop=True)
                    last.then_inc(s_rank_mm, 1)
                    pe.wait_ge(s_ranked, 2)
                if i == EG - 4:
                    pe.wait_ge(s_odd, 1)
                    pe.wait_ge(e_msged, i - 1)
                    T.matmul(bank[7][0:1, 0:1], ones128[:, 0:1], odd_sum[:], start=True, stop=True).then_inc(s_odd_mm, 1)
                    pe.wait_ge(s_general, 1)

            pe.wait_ge(s_const, 1)

            def hidden(i, m, t):
                if due(i):
                    pe.wait_ge(e_rlo, 4 * (i - 1) + t + 1)
                o = bank[2 + t][:]
                T.matmul(o, bias1[:, t, :], e_onehot[:, m % 4, :], start=True, stop=False)
                for k in range(2):
                    cols = slice((2 * t + k) * D, (2 * t + k + 1) * D)
                    last = product(o, w1_hi[:, cols], w1_lo[:, cols], e_h_hi[:, m % 2, k, :],
                                   e_h_lo[:, m % 2, k, :], False, k == 1)
                last.then_inc(e_l1, 1)

            def edge_step(i, m):
                g, s = i - 1, (m - 1) % 2
                if within(g, EG):
                    if due(g):
                        pe.wait_ge(e_msg_ted, g)
                    T.matmul(bank[6][:], bias2[:], e_onehot[:, (m - 1) % 4, :], start=True, stop=False)
                    for t in range(TYPES):
                        pe.wait_ge(e_rlo, 4 * g + t + 1)
                        last = product(bank[6][:], w2_hi[:, t * D:(t + 1) * D], w2_lo[:, t * D:(t + 1) * D],
                                       e_r_hi[:, s, t, :], e_r_lo[:, s, t, :], False, t == TYPES - 1)
                    last.then_inc(e_l2, 1)
                if within(i, EG):
                    pe.wait_ge(e_hlo, 2 * (i + 1))
                    pe.wait_ge(e_oh, i + 1)
                    for t in range(TYPES):
                        hidden(i, m, t)
                g, s = i + 1, (m + 1) % 2
                if within(g, EG):
                    pe.wait_ge(e_normed, g + 1)
                    if due(2 * g):
                        pe.wait_ge(e_hlo, 2 * g)
                    for k in range(2 * TILES):
                        last = T.transpose(bank[k // TILES][:, (k % TILES) * P:(k % TILES + 1) * P],
                                           e_h[:, s, k, :], ident[:])
                    last.then_inc(e_turned, 1)
                if isinstance(i, int):
                    find_starts(i)
                g, s = i - 1, (m - 1) % 2
                if within(g, EG):
                    pe.wait_ge(e_msg_ted, g + 1)
                    if due(g):
                        pe.wait_ge(e_msged, g)
                    for k in range(TILES):
                        last = T.transpose(bank[7][:, k * D:(k + 1) * D], e_msg_t[:, s, k * P:(k + 1) * P], ident[:])
                    last.then_inc(e_back, 1)

            pipeline(pe, EG, -1, 1, edge_step)

            pe.wait_ge(e_msged, EG)
            pe.wait_ge(s_gate_weights, 1)
            with pe.If(pe.value_load(general[:], min_val=0, max_val=1) > 0):
                with pe.Fori(0, ECOLS) as c:
                    pe.wait_ge(g_spread, c + 1)
                    T.transpose(bank[6][:, 0:P], g_dst[:, 0:P], ident[:]).then_inc(g_across, 1)
                    pe.wait_ge(g_samed, c + 1)
                    pe.wait_ge(g_summed, c + 1)
                    T.matmul(bank[7][:, 0:D], g_same[:, 0:P], g_msg[:, 0:D], start=True, stop=True).then_inc(g_added, 1)

            def gate(b, row, s, sources):
                cols = slice(row * D, (row + 1) * D)
                for n, source in enumerate(sources):
                    w_hi, w_lo, v_hi, v_lo = {"h": (whh_hi, whh_lo, n_h_hi, n_h_lo),
                                              "a": (wih_hi, wih_lo, n_a_hi, n_a_lo)}[source]
                    last = product(bank[b][:], w_hi[:, cols], w_lo[:, cols], v_hi[:, s, :], v_lo[:, s, :],
                                   n == 0, n == len(sources) - 1)
                last.then_inc(n_gate, 1)

            def node_step(i, m):
                if within(i, NG):
                    pe.wait_ge(n_hlo, i + 1)
                    pe.wait_ge(n_alo, i + 1)
                    if due(i):
                        pe.wait_ge(n_red, i)
                    gate(3, 0, m % 2, "ha")
                    if due(i):
                        pe.wait_ge(n_ted, i)
                    gate(4, 2, m % 2, "h")
                g, s = i + 1, (m + 1) % 2
                if within(g, NG):
                    pe.wait_ge(n_normed, g + 1)
                    if due(g - 1):
                        pe.wait_ge(n_ded, g - 1)
                    for k in range(TILES):
                        last = T.transpose(bank[s][:, k * P:(k + 1) * P], n_h[:, s, k * D:(k + 1) * D], ident[:])
                    last.then_inc(n_turned, 1)
                    pe.wait_ge(n_seled, g + 1)
                    pe.wait_ge(n_seled_pool, g + 1)
                    if due(g):
                        pe.wait_ge(n_alo, g)
                    for k in range(TILES):
                        last = T.matmul(bank[2][:, k * P:(k + 1) * P], n_win[:, (m + 1) % 4, k, 0:D],
                                        n_sel[:, s, k * P:(k + 1) * P], start=True, stop=True)
                    last.then_inc(n_summed, 1)
                if within(i, NG):
                    if due(i):
                        pe.wait_ge(n_ued, i)
                    gate(5, 2, m % 2, "a")
                    if due(i):
                        pe.wait_ge(n_zed, i)
                    gate(6, 1, m % 2, "ha")
                g, s = i - 1, (m - 1) % 2
                if within(g, NG):
                    pe.wait_ge(n_eed, g + 1)
                    if due(g):
                        pe.wait_ge(n_outed, g)
                    for k in range(TILES):
                        last = T.transpose(bank[7][:, k * P:(k + 1) * P], n_e[:, s, k * P:(k + 1) * P], ident[:])
                    last.then_inc(n_back, 1)

            pipeline(pe, NG, -1, 1, node_step)


def kernel(**inputs):
    import numpy as np
    import concourse.bacc as bacc
    from concourse.bass_utils import run_bass_kernel_spmd

    src, dst, types = (np.asarray(inputs[n]) for n in ("src", "dst", "edge_type_4"))
    edges = src.shape[0]
    eg = groups_of(edges)
    padded = np.zeros((3, eg * GROUP), np.int32)
    padded[0, :edges], padded[1, :edges], padded[2, :edges] = src, dst, types
    dst_marked = np.full(eg * GROUP + 1, groups_of(inputs["x"].shape[0]) * GROUP, np.int32)
    dst_marked[:edges] = dst
    arrays = {
        "x": np.ascontiguousarray(inputs["x"]),
        "edge_rows": np.ascontiguousarray(
            padded[0:2].reshape(2, eg, TILES, P).transpose(3, 1, 0, 2).reshape(P, eg, 2 * TILES)),
        "dst_cols": np.ascontiguousarray(dst_marked[:-1].reshape(eg * TILES, P).T),
        "dst_flat": dst_marked,
        "types": padded[2:3],
        "W1": np.ascontiguousarray(inputs["L0_gnn_W1"]),
        "b1": np.ascontiguousarray(inputs["L0_gnn_b1"]),
        "W2": np.ascontiguousarray(inputs["L0_gnn_W2"]),
        "b2": np.ascontiguousarray(inputs["L0_gnn_b2"]),
        "WihT": np.ascontiguousarray(np.asarray(inputs["L0_gnn_W_ih"]).T),
        "WhhT": np.ascontiguousarray(np.asarray(inputs["L0_gnn_W_hh"]).T),
        "b_ih": np.ascontiguousarray(np.asarray(inputs["L0_gnn_b_ih"]).reshape(3, D).T),
        "b_hh": np.ascontiguousarray(np.asarray(inputs["L0_gnn_b_hh"]).reshape(3, D).T),
    }
    nc = bacc.Bacc("TRN2", target_bir_lowering=False, num_devices=1)
    args = [nc.dram_tensor(f"in_{name}", a.shape, mybir.dt.from_np(a.dtype), kind="ExternalInput").ap()
            for name, a in arrays.items()]
    out = nc.dram_tensor("out_0", arrays["x"].shape, F32, kind="ExternalOutput").ap()
    gnn_layer(nc, *args, out)
    r = run_bass_kernel_spmd(nc, [{f"in_{name}": a for name, a in arrays.items()}], core_ids=[0])
    return r.results[0]["out_0"]
```
